# Optimizing a Trainium2 kernel written in Bass

```python
import numpy as np
import jax
import jax.numpy as jnp

def _softmax(x, axis=-1):
    return jax.nn.softmax(x, axis=axis)

def _gelu(x):
    return jax.nn.gelu(x, approximate=True)

def _silu(x):
    return jax.nn.silu(x)

def _sigmoid(x):
    return jax.nn.sigmoid(x)

def _layernorm(x, axis=-1, eps=1e-05):
    m = jnp.mean(x, axis=axis, keepdims=True)
    v = jnp.var(x, axis=axis, keepdims=True)
    return (x - m) / jnp.sqrt(v + eps)

def _scatter_add(tgt, idx, src, axis=0):
    return tgt.at[idx].add(src)

def _segment_sum(src, seg, n):
    return jax.ops.segment_sum(src, seg, n)
kernel_name = 'mk_vit_tower_postln_d1_tok_img1024_r4_bcb6dd'

def setup_inputs(seed: int=0):
    np.random.seed(seed)
    _w = jnp.asarray

    def _rec_inputs():
        import jax
        import jax.numpy as jnp
        _rk = jax.random.key(seed)
        x = -0.00016672 + 0.999947 * jax.random.normal(jax.random.fold_in(_rk, 1), (16, 3, 96, 96), jnp.float32)
        return x
    x = _rec_inputs()

    def _L0_tok_setup():
        import jax, jax.numpy as jnp
        import numpy as np
        EMBED_DIM = 256
        IMAGE_SIZE = 96
        CHANNELS = 3
        PATCH = 16
        NUM_PATCHES = (IMAGE_SIZE // PATCH) ** 2
        PATCH_DIM = PATCH * PATCH * CHANNELS

        def _patchify(x, patch):
            B, C, H, W = x.shape
            hp, wp = (H // patch, W // patch)
            x = x.reshape(B, C, hp, patch, wp, patch)
            x = x.transpose(0, 2, 4, 1, 3, 5)
            return x.reshape(B, hp * wp, C * patch * patch)
        key = jax.random.key(seed)
        k_x, k_w, k_b, k_cls, k_pos = jax.random.split(key, 5)
        x = jax.random.normal(k_x, (64, CHANNELS, IMAGE_SIZE, IMAGE_SIZE), dtype=jnp.float32)
        W = jax.random.normal(k_w, (EMBED_DIM, PATCH_DIM), dtype=jnp.float32) / np.sqrt(PATCH_DIM)
        b = jax.random.normal(k_b, (EMBED_DIM,), dtype=jnp.float32) * 0.01
        cls_token = jax.random.normal(k_cls, (1, 1, EMBED_DIM), dtype=jnp.float32)
        pos_embedding = jax.random.normal(k_pos, (1, 1 + NUM_PATCHES, EMBED_DIM), dtype=jnp.float32)
        return {'x': x, 'W': W, 'b': b, 'cls_token': cls_token, 'pos_embedding': pos_embedding}
    _L0_tok_all = _L0_tok_setup()
    _L0_tok_in = {k: v for k, v in _L0_tok_all.items() if k in ('W', 'b', 'cls_token', 'pos_embedding')}
    del _L0_tok_all

    def _L0_attn_setup():
        import jax, jax.numpy as jnp
        import numpy as np
        LN_EPS = 1e-05

        def _layernorm(x, g, b):
            mu = jnp.mean(x, axis=-1, keepdims=True)
            var = jnp.var(x, axis=-1, keepdims=True)
            return (x - mu) * jax.lax.rsqrt(var + LN_EPS) * g + b
        key = jax.random.key(seed)
        B, S, D, H = (2, 512, 256, 16)
        dh = D // H
        r = 48
        r_out = 192
        I = 4 * D
        r_mlp = 128
        ks = jax.random.split(key, 24)
        sc = lambda *sh: 0.02
        inp = {'hidden_states': jax.random.normal(ks[0], (B, S, D), jnp.float32), 'ln1_g': jnp.ones((D,), jnp.float32), 'ln1_b': jnp.zeros((D,), jnp.float32), 'ln2_g': jnp.ones((D,), jnp.float32), 'ln2_b': jnp.zeros((D,), jnp.float32), 'q_U': jax.random.normal(ks[1], (D, H, r), jnp.float32) * 0.02, 'q_V': jax.random.normal(ks[2], (H, r, dh), jnp.float32) * 0.02, 'q_b': jax.random.normal(ks[3], (H, dh), jnp.float32) * 0.02, 'k_U': jax.random.normal(ks[4], (D, H, r), jnp.float32) * 0.02, 'k_V': jax.random.normal(ks[5], (H, r, dh), jnp.float32) * 0.02, 'k_b': jax.random.normal(ks[6], (H, dh), jnp.float32) * 0.02, 'v_U': jax.random.normal(ks[7], (D, H, r), jnp.float32) * 0.02, 'v_V': jax.random.normal(ks[8], (H, r, dh), jnp.float32) * 0.02, 'v_b': jax.random.normal(ks[9], (H, dh), jnp.float32) * 0.02, 'out_U': jax.random.normal(ks[10], (D, r_out), jnp.float32) * 0.02, 'out_V': jax.random.normal(ks[11], (r_out, D), jnp.float32) * 0.02, 'out_b': jnp.zeros((D,), jnp.float32), 'fc1_U': jax.random.normal(ks[12], (D, r_mlp), jnp.float32) * 0.02, 'fc1_V': jax.random.normal(ks[13], (r_mlp, I), jnp.float32) * 0.02, 'fc1_b': jnp.zeros((I,), jnp.float32), 'fc2_U': jax.random.normal(ks[14], (I, r_mlp), jnp.float32) * 0.02, 'fc2_V': jax.random.normal(ks[15], (r_mlp, D), jnp.float32) * 0.02, 'fc2_b': jnp.zeros((D,), jnp.float32)}
        return inp
    _L0_attn_all = _L0_attn_setup()
    _L0_attn_in = {k: v for k, v in _L0_attn_all.items() if k in ('ln1_g', 'ln1_b', 'ln2_g', 'ln2_b', 'q_U', 'q_V', 'q_b', 'k_U', 'k_V', 'k_b', 'v_U', 'v_V', 'v_b', 'out_U', 'out_V', 'out_b', 'fc1_U', 'fc1_V', 'fc1_b', 'fc2_U', 'fc2_V', 'fc2_b')}
    del _L0_attn_all

    def _L0_ffn_setup():
        import jax, jax.numpy as jnp
        import numpy as np
        S, B, D = (256, 2, 256)
        E, TOPK = (15, 3)
        F = 256
        FS = 512

        def _uinit(k, shape, out_dim):
            std = out_dim ** (-0.5)
            return jax.random.uniform(k, shape, jnp.float32, -std, std)
        key = jax.random.key(seed)
        ks = jax.random.split(key, 10)
        return {'x': jax.random.normal(ks[0], (S, B, D), jnp.float32), 'gate_w': jax.random.normal(ks[1], (E, D), jnp.float32) * D ** (-0.5), 'fc1_w': _uinit(ks[2], (E, 2 * F, D), 2 * F), 'fc1_b': _uinit(ks[3], (E, 2 * F), 2 * F), 'geglu_mult': jnp.ones((E, F), jnp.float32), 'fc2_w': _uinit(ks[4], (E, D, F), D), 'fc2_b': _uinit(ks[5], (E, D), D), 's_fc1_w': _uinit(ks[6], (2 * FS, D), 2 * FS), 's_fc1_b': _uinit(ks[7], (2 * FS,), 2 * FS), 's_geglu_mult': jnp.ones((FS,), jnp.float32), 's_fc2_w': _uinit(ks[8], (D, FS), D), 's_fc2_b': _uinit(ks[9], (D,), D)}
    _L0_ffn_all = _L0_ffn_setup()
    _L0_ffn_in = {k: v for k, v in _L0_ffn_all.items() if k in ('gate_w', 'fc1_w', 'fc1_b', 'geglu_mult', 'fc2_w', 'fc2_b', 's_fc1_w', 's_fc1_b', 's_geglu_mult', 's_fc2_w', 's_fc2_b')}
    del _L0_ffn_all
    return {'x': x, 'L0_tok_W': _L0_tok_in['W'], 'L0_tok_b': _L0_tok_in['b'], 'L0_tok_cls_token': _L0_tok_in['cls_token'], 'L0_tok_pos_embedding': _L0_tok_in['pos_embedding'], 'L0_attn_ln1_g': _L0_attn_in['ln1_g'], 'L0_attn_ln1_b': _L0_attn_in['ln1_b'], 'L0_attn_ln2_g': _L0_attn_in['ln2_g'], 'L0_attn_ln2_b': _L0_attn_in['ln2_b'], 'L0_attn_q_U': _L0_attn_in['q_U'], 'L0_attn_q_V': _L0_attn_in['q_V'], 'L0_attn_q_b': _L0_attn_in['q_b'], 'L0_attn_k_U': _L0_attn_in['k_U'], 'L0_attn_k_V': _L0_attn_in['k_V'], 'L0_attn_k_b': _L0_attn_in['k_b'], 'L0_attn_v_U': _L0_attn_in['v_U'], 'L0_attn_v_V': _L0_attn_in['v_V'], 'L0_attn_v_b': _L0_attn_in['v_b'], 'L0_attn_out_U': _L0_attn_in['out_U'], 'L0_attn_out_V': _L0_attn_in['out_V'], 'L0_attn_out_b': _L0_attn_in['out_b'], 'L0_attn_fc1_U': _L0_attn_in['fc1_U'], 'L0_attn_fc1_V': _L0_attn_in['fc1_V'], 'L0_attn_fc1_b': _L0_attn_in['fc1_b'], 'L0_attn_fc2_U': _L0_attn_in['fc2_U'], 'L0_attn_fc2_V': _L0_attn_in['fc2_V'], 'L0_attn_fc2_b': _L0_attn_in['fc2_b'], 'L0_ffn_gate_w': _L0_ffn_in['gate_w'], 'L0_ffn_fc1_w': _L0_ffn_in['fc1_w'], 'L0_ffn_fc1_b': _L0_ffn_in['fc1_b'], 'L0_ffn_geglu_mult': _L0_ffn_in['geglu_mult'], 'L0_ffn_fc2_w': _L0_ffn_in['fc2_w'], 'L0_ffn_fc2_b': _L0_ffn_in['fc2_b'], 'L0_ffn_s_fc1_w': _L0_ffn_in['s_fc1_w'], 'L0_ffn_s_fc1_b': _L0_ffn_in['s_fc1_b'], 'L0_ffn_s_geglu_mult': _L0_ffn_in['s_geglu_mult'], 'L0_ffn_s_fc2_w': _L0_ffn_in['s_fc2_w'], 'L0_ffn_s_fc2_b': _L0_ffn_in['s_fc2_b']}

def reference(x, L0_tok_W, L0_tok_b, L0_tok_cls_token, L0_tok_pos_embedding, L0_attn_ln1_g, L0_attn_ln1_b, L0_attn_ln2_g, L0_attn_ln2_b, L0_attn_q_U, L0_attn_q_V, L0_attn_q_b, L0_attn_k_U, L0_attn_k_V, L0_attn_k_b, L0_attn_v_U, L0_attn_v_V, L0_attn_v_b, L0_attn_out_U, L0_attn_out_V, L0_attn_out_b, L0_attn_fc1_U, L0_attn_fc1_V, L0_attn_fc1_b, L0_attn_fc2_U, L0_attn_fc2_V, L0_attn_fc2_b, L0_ffn_gate_w, L0_ffn_fc1_w, L0_ffn_fc1_b, L0_ffn_geglu_mult, L0_ffn_fc2_w, L0_ffn_fc2_b, L0_ffn_s_fc1_w, L0_ffn_s_fc1_b, L0_ffn_s_geglu_mult, L0_ffn_s_fc2_w, L0_ffn_s_fc2_b):
    import jax
    import jax.numpy as jnp

    def _L0_tok_ref(x, W, b, cls_token, pos_embedding):
        import jax, jax.numpy as jnp
        import numpy as np
        EMBED_DIM = 256
        IMAGE_SIZE = 96
        CHANNELS = 3
        PATCH = 16
        NUM_PATCHES = (IMAGE_SIZE // PATCH) ** 2
        PATCH_DIM = PATCH * PATCH * CHANNELS

        def _patchify(x, patch):
            B, C, H, W = x.shape
            hp, wp = (H // patch, W // patch)
            x = x.reshape(B, C, hp, patch, wp, patch)
            x = x.transpose(0, 2, 4, 1, 3, 5)
            return x.reshape(B, hp * wp, C * patch * patch)
        B = x.shape[0]
        patches = _patchify(x, PATCH)
        tokens = jnp.einsum('bnd,ed->bne', patches, W) + b
        cls = jnp.broadcast_to(cls_token, (B, 1, EMBED_DIM))
        out = jnp.concatenate([cls, tokens], axis=1)
        return out + pos_embedding

    def _L0_attn_ref(hidden_states, ln1_g, ln1_b, ln2_g, ln2_b, q_U, q_V, q_b, k_U, k_V, k_b, v_U, v_V, v_b, out_U, out_V, out_b, fc1_U, fc1_V, fc1_b, fc2_U, fc2_V, fc2_b):
        import jax, jax.numpy as jnp
        import numpy as np
        LN_EPS = 1e-05

        def _layernorm(x, g, b):
            mu = jnp.mean(x, axis=-1, keepdims=True)
            var = jnp.var(x, axis=-1, keepdims=True)
            return (x - mu) * jax.lax.rsqrt(var + LN_EPS) * g + b
        B, S, D = hidden_states.shape
        H, dh = (q_V.shape[0], q_V.shape[2])
        x = _layernorm(hidden_states, ln1_g, ln1_b)
        Q = jnp.einsum('bsd,dhr,hre->bhse', x, q_U, q_V) + q_b[None, :, None, :]
        Pk = jnp.einsum('bsd,dhr->bhsr', x, k_U)
        Pv = jnp.einsum('bsd,dhr->bhsr', x, v_U)
        K = jnp.einsum('bhsr,hrd->bhsd', Pk, k_V) + k_b[None, :, None, :]
        V = jnp.einsum('bhsr,hrd->bhsd', Pv, v_V) + v_b[None, :, None, :]
        scale = 1.0 / jnp.sqrt(jnp.asarray(dh, x.dtype))
        scores = jnp.einsum('bhse,bhte->bhst', Q, K) * scale
        causal = jnp.tril(jnp.ones((S, S), bool))
        scores = jnp.where(causal[None, None], scores, jnp.asarray(-1000000000.0, scores.dtype))
        attn = jax.nn.softmax(scores, axis=-1)
        ctx = jnp.einsum('bhst,bhtd->bhsd', attn, V)
        ctx = ctx.transpose(0, 2, 1, 3).reshape(B, S, D)
        attn_out = ctx @ out_U @ out_V + out_b
        h = hidden_states + attn_out
        x2 = _layernorm(h, ln2_g, ln2_b)
        hmid = jax.nn.gelu(x2 @ fc1_U @ fc1_V + fc1_b, approximate=True)
        mlp_out = hmid @ fc2_U @ fc2_V + fc2_b
        return h + mlp_out

    def _L0_ffn_ref(x, gate_w, fc1_w, fc1_b, geglu_mult, fc2_w, fc2_b, s_fc1_w, s_fc1_b, s_geglu_mult, s_fc2_w, s_fc2_b):
        import jax, jax.numpy as jnp
        import numpy as np
        S, B, D = (256, 2, 256)
        E, TOPK = (15, 3)
        F = 256
        FS = 512

        def _uinit(k, shape, out_dim):
            std = out_dim ** (-0.5)
            return jax.random.uniform(k, shape, jnp.float32, -std, std)
        s, b, d = x.shape
        xt = x.reshape(-1, d)
        T = xt.shape[0]
        logits = xt @ gate_w.T
        scores = jax.nn.softmax(logits, axis=-1)
        topk_w, topk_idx = jax.lax.top_k(scores, TOPK)
        topk_w = topk_w / (jnp.sum(topk_w, axis=-1, keepdims=True) + 1e-20)
        comb = jnp.zeros((T, E), xt.dtype).at[jnp.arange(T)[:, None], topk_idx].add(topk_w)
        h = jnp.einsum('td,efd->etf', xt, fc1_w) + fc1_b[:, None, :]
        xh, g = (h[..., :F], h[..., F:])
        a = jax.nn.gelu(g, approximate=False) * xh * geglu_mult[:, None, :]
        yexp = jnp.einsum('etf,edf->etd', a, fc2_w) + fc2_b[:, None, :]
        y = jnp.einsum('etd,te->td', yexp, comb)
        hs = xt @ s_fc1_w.T + s_fc1_b
        xs, gs = (hs[..., :FS], hs[..., FS:])
        as_ = jax.nn.gelu(gs, approximate=False) * xs * s_geglu_mult
        ys = as_ @ s_fc2_w.T + s_fc2_b
        return (y + ys).reshape(s, b, d)
    h = _L0_tok_ref(x, L0_tok_W, L0_tok_b, L0_tok_cls_token, L0_tok_pos_embedding)
    h = _layernorm(h + _L0_attn_ref(h, L0_attn_ln1_g, L0_attn_ln1_b, L0_attn_ln2_g, L0_attn_ln2_b, L0_attn_q_U, L0_attn_q_V, L0_attn_q_b, L0_attn_k_U, L0_attn_k_V, L0_attn_k_b, L0_attn_v_U, L0_attn_v_V, L0_attn_v_b, L0_attn_out_U, L0_attn_out_V, L0_attn_out_b, L0_attn_fc1_U, L0_attn_fc1_V, L0_attn_fc1_b, L0_attn_fc2_U, L0_attn_fc2_V, L0_attn_fc2_b), axis=-1)
    h = _layernorm(h + _L0_ffn_ref(h, L0_ffn_gate_w, L0_ffn_fc1_w, L0_ffn_fc1_b, L0_ffn_geglu_mult, L0_ffn_fc2_w, L0_ffn_fc2_b, L0_ffn_s_fc1_w, L0_ffn_s_fc1_b, L0_ffn_s_geglu_mult, L0_ffn_s_fc2_w, L0_ffn_s_fc2_b), axis=-1)
    return h

_drawn_inputs = setup_inputs


def setup_inputs(seed=0):
    import zlib

    import numpy as np

    out = dict(_drawn_inputs(seed))
    spreads = {'L0_attn_ln1_g': (1.0, 0.6),
     'L0_attn_ln1_b': (0.0, 0.8),
     'L0_attn_ln2_g': (1.0, 0.6),
     'L0_attn_ln2_b': (0.0, 0.8),
     'L0_attn_out_b': (0.0, 2.0),
     'L0_attn_fc1_b': (0.0, 0.8),
     'L0_attn_fc2_b': (0.0, 2.0),
     'L0_ffn_geglu_mult': (1.0, 0.6),
     'L0_ffn_s_geglu_mult': (1.0, 0.6)}
    factors = {'L0_tok_b': 7.407,
     'L0_attn_q_U': 8.0,
     'L0_attn_q_V': 8.0,
     'L0_attn_q_b': 8.0,
     'L0_attn_k_U': 8.0,
     'L0_attn_k_V': 8.0,
     'L0_attn_k_b': 200.0,
     'L0_attn_v_U': 8.0,
     'L0_attn_v_V': 8.0,
     'L0_attn_v_b': 8.0,
     'L0_attn_out_U': 8.0,
     'L0_attn_out_V': 8.0,
     'L0_attn_fc1_U': 8.0,
     'L0_attn_fc1_V': 8.0,
     'L0_attn_fc2_U': 8.0,
     'L0_attn_fc2_V': 8.0,
     'L0_ffn_fc1_b': 8.0,
     'L0_ffn_s_fc1_b': 8.0}
    for name, (base, spread) in spreads.items():
        noise = np.random.default_rng([zlib.crc32(name.encode()), seed]).standard_normal(out[name].shape)
        drawn = base * np.exp(spread * noise) if base else spread * noise
        out[name] = jnp.asarray(drawn.astype(out[name].dtype))
    for name, factor in factors.items():
        out[name] = (out[name] * factor).astype(out[name].dtype)
    return out
```

```python
from contextlib import ExitStack

import numpy as np
import concourse.bass as bass
from concourse import mybir

F32 = mybir.dt.float32
F32R = mybir.dt.float32r
BF16 = mybir.dt.bfloat16
ACT = mybir.ActivationFunctionType
ALU = mybir.AluOpType
AX = mybir.AxisListType

P = 128
B, CH, IMG, PATCH = 16, 3, 96, 16
NPATCH = (IMG // PATCH) ** 2
S = NPATCH + 1
T = B * S
NH = 2
HB = B // NH
HT = T // NH
HP = HB * NPATCH
D = 256
DC = D // P
KP = CH * PATCH * PATCH // P
H, DH, R = 16, 16, 48
HC = P // DH
R_OUT, RO = 192, 96
R_MLP = 128
FI = 4 * D
FIC = FI // P
E, TOPK, F, FS = 15, 3, 256, 512
NS = FS // F
NE = NS + E
W1C, W2C = DC * 2 * F, F // P * D
SMALL = 3 * (F // P)
EXP_COLS = W1C + W2C + SMALL
G3 = 3
NG = (H + G3 - 1) // G3
PAIRS = B // 2
QB = 64
QROWS = QB + S
TT = 5
LAST = T - (TT - 1) * P
TPAD = TT * P
EPS = 1e-5
GATE_STEPS = 9
LOG_COLS = 20

_v = 0


def _col(n):
    global _v
    _v += n
    return _v - n


C_TOKB, C_POS, C_CLS = _col(DC), _col(DC * S), _col(DC)
C_LN1G, C_LN1B, C_LN2G, C_LN2B = _col(DC), _col(DC), _col(DC), _col(DC)
C_QB, C_KB, C_VB, C_OUTB = _col(DC), _col(DC), _col(DC), _col(DC)
C_FC1B, C_FC2B = _col(FIC), _col(DC)
NVEC = _v
_v = 0
C_ID, C_ONES, C_BLK, C_M3, C_CAUS = _col(P), _col(P), _col(HC), _col(D), _col(HC * S)
NCST = _v


def vit_tower_kernel(nc, patches, tok_w, vecs, csts, ut, vblk, out_u, out_v, fc1_u, fc1_v, fc2_u, fc2_v,
                     gate, experts, b2, out, comb_dram):
    ctx = ExitStack()
    with ctx:
        def sb(name, shape, dt=F32):
            return ctx.enter_context(nc.sbuf_tensor(name, shape, dt))

        def sem(name):
            return ctx.enter_context(nc.semaphore(name))

        pt_mem = sb("patches_sb", [P, KP * B * NPATCH])
        pt_sb = pt_mem[:, :].rearrange("p (k n) -> p k n", k=KP)
        tw_mem = sb("tok_w_sb", [P, KP * D])
        tw_sb = tw_mem[:, :].rearrange("p (k n) -> p k n", k=KP)
        vec = sb("vec_sb", [P, NVEC])
        cst = sb("cst_sb", [P, NCST])
        ident, ones_d = cst[:, C_ID:C_ID + P], cst[:, C_ONES:C_ONES + P]
        eps_t = sb("eps_t", [P, 1])
        zero_t = sb("zero_t", [P, 1])
        ident_bf = sb("ident_bf", [P, S], BF16)
        caus_bf = sb("caus_bf", [P, HC * S], BF16)
        h0 = sb("h0", [P, DC, T])
        xn = sb("xn", [P, DC, T])
        qT = sb("qT", [P, DC, T])
        kT = sb("kT", [P, DC, T])
        h3 = sb("h3", [P, DC, T])
        ut_mem = sb("ut_sb", [P, 3 * H // 2 * D])
        ut_sb = ut_mem[0:2 * R, :].rearrange("p (i j d) -> p i j d", i=3, j=H // 2)
        vb_sb = sb("vb_sb", [2 * R, 3, H // 2, 2 * DH])
        wqkv = sb("wqkv", [P, 3, DC, D])
        ou_sb = sb("ou_sb", [RO, 2, D])
        ov_sb = sb("ov_sb", [RO, 2, D])
        wo = sb("wo", [P, DC, D])
        xc = sb("ln_xc", [P, NH, DC, HT])
        sq = sb("ln_sq", [P, NH, DC, HT])
        sd = sb("ln_sd", [P, NH, HT])
        rs = sb("ln_rs", [P, NH, HT])
        qst = sb("qst", [P, 2, DC, 2 * S])
        xst = sb("xst", [P, 2, DC, 2, G3 * S])
        dsc = sb("dsc", [P, 2, H, S])
        prob = sb("prob", [P, 2, H, S])
        mx = sb("mx", [P, 2, H])
        sm = sb("sm", [P, 2, H])
        rsm = sb("rsm", [P, 2, H])
        pT = sb("pT", [G3 * S, NG, QROWS])
        v3 = sb("v3", [G3 * S, 2, D])
        cx = sb("cx", [P, H, DH])
        f1u = sb("f1u", [P, DC, R_MLP])
        f1v = sb("f1v", [P, FI])
        f2u = sb("f2u", [P, FIC, R_MLP])
        f2v = sb("f2v", [P, D])
        gw = sb("gw", [P, DC, E])
        lg = sb("lg", [P, TT, LOG_COLS])
        top = sb("top", [P, TT, 8])
        rep = sb("rep", [P, TT, LOG_COLS])
        g1 = sb("g1", [P, TT])
        g2 = sb("g2", [P, TT])
        comb = sb("comb", [P, TT, 32])
        combT = sb("combT", [P, TT, 32])
        comb17 = sb("comb17", [NE, T])
        b2_sb = sb("b2_sb", [NE, D])
        x_hi = sb("x_hi", [P, DC, T], F32R)
        x_lo = sb("x_lo", [P, DC, T], F32R)
        stage = sb("stage", [P, 2, EXP_COLS])
        small = sb("small", [P, 2, SMALL])
        w_hi = sb("w_hi", [P, 2, W1C + W2C], F32R)
        w_lo = sb("w_lo", [P, 2, W1C + W2C], F32R)
        cb = sb("cb", [P, 2, T])
        ones_t = sb("ones_t", [P, HT])
        t1 = sb("t1", [P, 2, HT])
        t2 = sb("t2", [P, 2, HT])
        a_hi = sb("a_hi", [P, 4, HT], F32R)
        a_lo = sb("a_lo", [P, 4, HT], F32R)

        at = 2 * 2 * DC * HC * S
        kblk = ut_mem[:, 0:at].rearrange("p (a u c h s) -> p a u c h s", a=2, u=2, c=DC, h=HC)
        cT, h1, hs = (ut_mem[:, at + i * DC * T:at + (i + 1) * DC * T].rearrange("p (c t) -> p c t", c=DC)
                      for i in range(3))
        hm = pt_mem[:, 0:FIC * HT].rearrange("p (f t) -> p f t", f=FIC)
        gel = pt_mem[:, FIC * HT:(FIC + 2) * HT].rearrange("p (j t) -> p j t", j=2)
        z1 = tw_mem[:, 0:T].rearrange("p (n t) -> p n t", n=NH)
        z2 = tw_mem[:, T:2 * T].rearrange("p (n t) -> p n t", n=NH)

        ps = ctx.enter_context(nc.psum_tensor("ps", [P, 8, 512], F32))

        ld_patch = [sem(f"ld_patch{k}") for k in range(KP)]
        ld_cst, ld_vec, ld_out = sem("ld_cst"), sem("ld_vec"), sem("ld_out_w")
        ld_qkv = [sem(f"ld_qkv{i}") for i in range(3)]
        ld_mlp, ld_gate, ld_b2 = sem("ld_mlp"), sem("ld_gate"), sem("ld_b2")
        ld_exp = [sem("ld_exp0"), sem("ld_exp1")]
        ld_cb = [sem("ld_cb0"), sem("ld_cb1")]
        ld_c17 = sem("ld_c17")
        st_comb, st_out = sem("st_comb"), sem("st_out")
        init_done = sem("init_done")
        psum_clear = sem("psum_clear")
        emb_mm, emb_done = sem("emb_mm"), sem("emb_done")
        cmp_mm, cmp_done = sem("cmp_mm"), sem("cmp_done")
        qk_mm, q_done, k_done = sem("qk_mm"), sem("q_done"), sem("k_done")
        staged = sem("staged")
        s_mm, s_max, s_cen, s_exp, s_sum, s_rec = (sem(n) for n in ("s_mm", "s_max", "s_cen", "s_exp", "s_sum", "s_rec"))
        v_mm, v_done, tr_mm, tr_done = sem("v_mm"), sem("v_done"), sem("tr_mm"), sem("tr_done")
        pv_mm, cx_done, ct_mm, ct_done = sem("pv_mm"), sem("cx_done"), sem("ct_mm"), sem("ct_done")
        op_mm, op_done = sem("op_mm"), sem("op_done")
        sum_done = sem("sum_done")
        z1_mm, z1_done, hm_mm, hm_done = sem("z1_mm"), sem("z1_done"), sem("hm_mm"), sem("hm_done")
        z2_mm, z2_done, mo_mm, mo_done = sem("z2_mm"), sem("z2_done"), sem("mo_mm"), sem("mo_done")
        lg_mm, gt, top_done = sem("lg_mm"), sem("gate_chain"), sem("top_done")
        gt_exp = sem("gate_exp")
        xs_hi, xs_lo = sem("xs_hi"), sem("xs_lo")
        w1_hi_done, w2_hi_done, w1_lo_done, w2_lo_done = sem("w1_hi"), sem("w2_hi"), sem("w1_lo"), sem("w2_lo")
        small_done = sem("small_done")
        g_mm, x_mm, gel_done, t1_done, t2_done = sem("g_mm"), sem("x_mm"), sem("gel_done"), sem("t1_done"), sem("t2_done")
        ah_done, al_done, y_mm = sem("ah_done"), sem("al_done"), sem("y_mm")
        y_fin, y_done = sem("y_fin"), sem("y_done")

        class Norm:

            def __init__(self, name, mean_bank, var_bank):
                self.mean_bank, self.var_bank = mean_bank, var_bank
                self.mean, self.cen, self.sq = sem(name + "_mean"), sem(name + "_cen"), sem(name + "_sq")
                self.var, self.sd, self.rs = sem(name + "_var"), sem(name + "_sd"), sem(name + "_rs")
                self.out, self.aff = sem(name + "_out"), sem(name + "_aff")

        ln1, ln2, ln3, ln4 = Norm("ln1", 4, 6), Norm("ln2", 4, 6), Norm("ln3", 0, 4), Norm("ln4", 4, 6)

        def half(t, n):
            return t[:, :, n * HT:(n + 1) * HT]

        def mm(o, w, x, start=True, stop=True):
            return nc.tensor.matmul(o, w, x, start=start, stop=stop)

        def weight3(w, o, w_h, w_l, x_h, x_l, first, last):
            mm(o, w(w_h), x_h, start=first, stop=False)
            mm(o, w(w_h), x_l, start=False, stop=False)
            return mm(o, w(w_l), x_h, start=False, stop=last)

        def over_pairs(fori, ahead, rest):
            ahead(0, 0)
            ahead(1, 1)
            rest(0, 0)
            with fori(0, (PAIRS - 2) // 2) as i:
                ahead(i * 2 + 2, 0)
                rest(i * 2 + 1, 1)
                ahead(i * 2 + 3, 1)
                rest(i * 2 + 2, 0)
            rest(PAIRS - 1, 1)

        def after(eng, semaphore, count):
            if not (isinstance(count, int) and count == 0):
                eng.wait_ge(semaphore, count)

        def over_experts(fori, expert):
            expert(0, 0, 0)
            expert(1, 1, 0)
            with fori(0, (NE - 3) // 2) as i:
                expert(i * 2 + 2, 0, i + 1)
                expert(i * 2 + 3, 1, i + 1)
            expert(NE - 1, 0, (NE - 1) // 2)

        block = ctx.enter_context(nc.Block())

        @block.sync
        def _(sp):
            sp.dma_start(cst[:, :], csts).then_inc(ld_cst, 16)
            sp.dma_start(vec[:, :], vecs).then_inc(ld_vec, 16)
            for k in range(KP):
                sp.dma_start(tw_sb[:, k], tok_w[:, k]).then_inc(ld_patch[k], 16)
                sp.dma_start(pt_sb[:, k], patches[:, k]).then_inc(ld_patch[k], 16)
            for i in range(3):
                sp.dma_start(ut_sb[:, i], ut[:, i]).then_inc(ld_qkv[i], 16)
                sp.dma_start(vb_sb[:, i], vblk[:, i]).then_inc(ld_qkv[i], 16)
            sp.dma_start(ou_sb[:, :], out_u).then_inc(ld_out, 16)
            sp.dma_start(ov_sb[:, :], out_v).then_inc(ld_out, 16)
            sp.dma_start(f1u[:, :], fc1_u).then_inc(ld_mlp, 16)
            sp.dma_start(f1v[:, :], fc1_v).then_inc(ld_mlp, 16)
            sp.dma_start(f2u[:, :], fc2_u).then_inc(ld_mlp, 16)
            sp.dma_start(f2v[:, :], fc2_v).then_inc(ld_mlp, 16)
            sp.dma_start(gw[:, :], gate).then_inc(ld_gate, 16)
            sp.dma_start(b2_sb[:, :], b2).then_inc(ld_b2, 16)

            def expert(e, par, turn):
                if not (isinstance(e, int) and e < 2):
                    sp.wait_ge(small_done, e - 1)
                sp.dma_start(stage[:, par], experts[bass.ds(e * P, P), :]).then_inc(ld_exp[par], 16)
                if isinstance(e, int) and e == 1:
                    sp.wait_ge(gt, GATE_STEPS)
                    for q in range(4):
                        rows = comb_dram.rearrange("e (t q c) -> e t q c", q=4, c=32)[:, :, q, :]
                        sp.dma_start(rows, combT[32 * q:32 * q + NE, :, :]).then_inc(st_comb, 16)
                    sp.wait_ge(st_comb, 64)
                    sp.dma_start(comb17[:, :], comb_dram[:, 0:T]).then_inc(ld_c17, 16)
                if not (isinstance(e, int) and e < 2):
                    sp.wait_ge(t2_done, 4 * (e - 1))
                    sp.dma_start(cb[:, par], comb_dram[bass.ds(e, 1), 0:T].to_broadcast([P, T])) \
                        .then_inc(ld_cb[par], 16)

            over_experts(sp.Fori, expert)

            for n in range(NH):
                sp.wait_ge(ln4.out, n + 1)
                for c in range(DC):
                    sp.dma_start(out[c * P:(c + 1) * P, n * HT:(n + 1) * HT], sq[:, n, c]).then_inc(st_out, 16)
            sp.wait_ge(st_out, 16 * NH * DC)

        @block.gpsimd
        def _(pool):
            def ahead(p, par):
                if isinstance(p, int) and p == 0:
                    pool.wait_ge(q_done, 4)
                    pool.wait_ge(k_done, 4)
                if not (isinstance(p, int) and p < 2):
                    pool.wait_ge(s_mm, p - 1)
                    pool.wait_ge(v_mm, p - 1)
                t0 = p * (2 * S)
                for u in range(2):
                    kv = kT[:, :, bass.ds(t0 + u * S, S)]
                    for c in range(DC):
                        last = pool.tensor_tensor(
                            kblk[:, par, u, c], kv[:, c].unsqueeze(1).to_broadcast([P, HC, S]),
                            cst[:, C_BLK:C_BLK + HC].unsqueeze(2).to_broadcast([P, HC, S]), ALU.mult)
                        last.then_inc(staged, 1)
                pool.tensor_copy(qst[:, par], qT[:, :, bass.ds(t0, 2 * S)]).then_inc(staged, 1)
                for c in range(DC):
                    pool.tensor_copy(
                        xst[:, par, c].rearrange("p u (r s) -> p u r s", r=G3),
                        xn[:, c, bass.ds(t0, 2 * S)].rearrange("p (u s) -> p u s", u=2).unsqueeze(2)
                        .to_broadcast([P, 2, G3, S])).then_inc(staged, 1)

            over_pairs(pool.Fori, ahead, lambda p, par: None)

            for n in range(NH):
                pool.wait_ge(op_done, DC * (n + 1))
                pool.tensor_tensor(half(hs, n), half(h0, n), half(h1, n), ALU.add).then_inc(sum_done, 1)

            def split_lo(e, par, turn):
                pool.wait_ge(w1_hi_done, e + 1)
                if not (isinstance(e, int) and e < 2):
                    pool.wait_ge(x_mm, 4 * (e - 1))
                pool.tensor_tensor(w_lo[:, par, 0:W1C], stage[:, par, 0:W1C],
                                   w_hi[:, par, 0:W1C].bitcast(F32), ALU.subtract).then_inc(w1_lo_done, 1)
                pool.wait_ge(w2_hi_done, e + 1)
                if not (isinstance(e, int) and e < 2):
                    pool.wait_ge(y_mm, 4 * (e - 1))
                pool.tensor_tensor(w_lo[:, par, W1C:W1C + W2C], stage[:, par, W1C:W1C + W2C],
                                   w_hi[:, par, W1C:W1C + W2C].bitcast(F32), ALU.subtract).then_inc(w2_lo_done, 1)
                pool.tensor_copy(small[:, par], stage[:, par, W1C + W2C:EXP_COLS]).then_inc(small_done, 1)

            over_experts(pool.Fori, split_lo)

        @block.scalar
        def _(act):
            def norm_act(ln, n):
                act.wait_ge(ln.cen, n + 1)
                nc.scalar.activation(sq[:, n], xc[:, n], ACT.Square).then_inc(ln.sq, 1)
                act.wait_ge(ln.var, n + 1)
                nc.scalar.activation(sd[:, n], ps[:, ln.var_bank + n, 0:HT], ACT.Sqrt,
                                     bias=eps_t[:, 0:1]).then_inc(ln.sd, 1)

            def affine_act(ln, n, gamma, beta):
                act.wait_ge(ln.out, n + 1)
                for c in range(DC):
                    nc.scalar.activation(xn[:, c, n * HT:(n + 1) * HT], sq[:, n, c], ACT.Identity,
                                         bias=vec[:, beta + c:beta + c + 1],
                                         scale=vec[:, gamma + c:gamma + c + 1]).then_inc(ln.aff, 1)

            act.wait_ge(ld_vec, 16)
            act.wait_ge(init_done, 2)
            norm_act(ln1, 0)
            norm_act(ln1, 1)
            for i in range(4):
                act.wait_ge(cmp_mm, i + 1)
                nc.scalar.activation(wqkv[:, i].rearrange("p c d -> p (c d)") if i < 3
                                     else wo[:, :].rearrange("p c d -> p (c d)"),
                                     ps[:, i, :], ACT.Copy).then_inc(cmp_done, 1)
            affine_act(ln1, 0, C_LN1G, C_LN1B)
            affine_act(ln1, 1, C_LN1G, C_LN1B)
            for n in range(NH):
                for c in range(DC):
                    act.wait_ge(qk_mm, 4 * n + c + 1)
                    nc.scalar.activation(qT[:, c, n * HT:(n + 1) * HT], ps[:, 4 * (1 - n) + c, 0:HT],
                                         ACT.Identity, bias=vec[:, C_QB + c:C_QB + c + 1]).then_inc(q_done, 2)

            def rest(p, par):
                act.wait_ge(s_cen, p * 2 + 2)
                nc.scalar.activation(prob[0:QROWS, par], dsc[0:QROWS, par], ACT.Exp,
                                     scale=DH ** -0.5).then_inc(s_exp, 1)
                act.wait_ge(tr_mm, p + 1)
                after(act, pv_mm, p)
                for k in range(2):
                    nc.scalar.activation(pT[:, k * G3:(k + 1) * G3].rearrange("p g q -> p (g q)"),
                                         ps[0:G3 * S, 4 + k, 0:G3 * QROWS], ACT.Copy).then_inc(tr_done, 1)
                act.wait_ge(ct_mm, p + 1)
                for c in range(DC):
                    nc.scalar.activation(
                        cT[:, c, bass.ds(p * (2 * S), 2 * S)].rearrange("p (u s) -> p u s", u=2),
                        ps[:, 7, 256 + c * P:256 + (c + 1) * P].rearrange("p (u s) -> p u s", u=2)[:, :, 0:S],
                        ACT.Identity, bias=vec[:, C_VB + c:C_VB + c + 1]).then_inc(ct_done, 1)

            over_pairs(act.Fori, lambda p, par: None, rest)

            norm_act(ln2, 0)
            norm_act(ln2, 1)
            affine_act(ln2, 0, C_LN2G, C_LN2B)
            affine_act(ln2, 1, C_LN2G, C_LN2B)
            for n in range(NH):
                for f in range(FIC):
                    act.wait_ge(hm_mm, FIC * n + f + 1)
                    if n == 1 and f == 0:
                        act.wait_ge(z2_mm, 1)
                    nc.scalar.activation(hm[:, f], ps[:, 2 + f % 2, 0:HT], ACT.Gelu_apprx_tanh,
                                         bias=vec[:, C_FC1B + f:C_FC1B + f + 1]).then_inc(hm_done, 1)
            norm_act(ln3, 0)
            norm_act(ln3, 1)
            for n in range(NH):
                act.wait_ge(ln3.aff, n + 1)
                nc.scalar.activation(half(x_hi, n), half(h3, n), ACT.Copy).then_inc(xs_hi, 1)

            def w1_hi(e, par, turn):
                act.wait_ge(ld_exp[par], 16 * (turn + 1))
                if not (isinstance(e, int) and e < 2):
                    act.wait_ge(x_mm, 4 * (e - 1))
                nc.scalar.activation(w_hi[:, par, 0:W1C], stage[:, par, 0:W1C], ACT.Copy).then_inc(w1_hi_done, 1)

            def w2_hi(e, par, turn):
                if not (isinstance(e, int) and e < 2):
                    act.wait_ge(y_mm, 4 * (e - 1))
                nc.scalar.activation(w_hi[:, par, W1C:W1C + W2C], stage[:, par, W1C:W1C + W2C],
                                     ACT.Copy).then_inc(w2_hi_done, 1)

            w1_hi(0, 0, 0)
            w2_hi(0, 0, 0)
            w1_hi(1, 1, 0)
            w2_hi(1, 1, 0)
            act.wait_ge(gt, 2)
            nc.scalar.activation(lg[:, :, 0:E], lg[:, :, 0:E], ACT.Exp).then_inc(gt_exp, 1)

            def act_hi(k, u):
                act.wait_ge(t2_done, k + 1)
                if not (isinstance(k, int) and k < 4):
                    act.wait_ge(y_mm, k - 3)
                nc.scalar.activation(a_hi[:, u], t2[:, u % 2], ACT.Copy).then_inc(ah_done, 1)

            def expert(e, par, turn):
                for u in range(4):
                    k = e * 4 + u
                    j = u % 2
                    act.wait_ge(g_mm, k + 1)
                    if not (isinstance(k, int) and k < 2):
                        act.wait_ge(t1_done, k - 1)
                    if u == 0:
                        act.wait_ge(small_done, e + 1)
                    nc.scalar.activation(gel[:, u % 2], ps[:, 4 + 2 * (u % 2), 0:HT], ACT.Gelu,
                                         bias=small[:, par, j:j + 1]).then_inc(gel_done, 1)
                    if not (isinstance(k, int) and k == 0):
                        act_hi(k - 1, (u - 1) % 4)
                    more = not (isinstance(e, int) and (e == 0 or e == NE - 1))
                    if u == 0 and more:
                        w1_hi(e + 1, 1 - par, turn + par)
                    if u == 2 and more:
                        w2_hi(e + 1, 1 - par, turn + par)

            over_experts(act.Fori, expert)
            act_hi(4 * NE - 1, 3)
            norm_act(ln4, 0)
            norm_act(ln4, 1)

        @block.vector
        def _(dve):
            nc.vector.memset(eps_t[:, :], EPS).then_inc(init_done, 1)
            nc.vector.memset(ones_t[:, :], 1.0).then_inc(init_done, 1)
            nc.vector.memset(ps[:, 4:8, :], 0.0).then_inc(psum_clear, 1)
            nc.vector.memset(comb[:, :, :], 1.0).then_inc(init_done, 1)
            nc.vector.memset(lg[:, :, :], -1.0).then_inc(init_done, 1)
            dve.wait_ge(ld_cst, 16)
            nc.vector.tensor_copy(ident_bf[:, :], cst[:, C_ID:C_ID + S]).then_inc(init_done, 1)
            nc.vector.tensor_copy(caus_bf[:, :], cst[:, C_CAUS:C_CAUS + HC * S]).then_inc(init_done, 1)
            dve.wait_ge(ld_vec, 16)
            pos = vec[:, C_POS:C_POS + DC * S].rearrange("p (c s) -> p c s", c=DC)
            for c in range(DC):
                hv = h0[:, c, :].rearrange("p (b s) -> p b s", b=B)
                nc.vector.tensor_scalar(hv[:, :, 0], pos[:, c, 0:1].to_broadcast([P, B]),
                                        vec[:, C_CLS + c:C_CLS + c + 1], None, ALU.add).then_inc(emb_done, 1)
            for n in range(NH):
                for c in range(DC):
                    dve.wait_ge(emb_mm, 2 * n + c + 1)
                    hv = h0[:, c, :].rearrange("p (b s) -> p b s", b=B)
                    nc.vector.scalar_tensor_tensor(
                        hv[:, n * HB:(n + 1) * HB, 1:S],
                        ps[:, 2 * n + c, 0:HP].rearrange("p (b s) -> p b s", b=HB),
                        vec[:, C_TOKB + c:C_TOKB + c + 1],
                        pos[:, c, 1:S].unsqueeze(1).to_broadcast([P, HB, NPATCH]),
                        ALU.add, ALU.add).then_inc(emb_done, 1)

            def centre(ln, n, src):
                dve.wait_ge(ln.mean, n + 1)
                nc.vector.tensor_tensor(
                    xc[:, n], half(src, n),
                    ps[:, ln.mean_bank + n, 0:HT].unsqueeze(1).to_broadcast([P, DC, HT]),
                    ALU.subtract).then_inc(ln.cen, 1)

            def scale(ln, n, dst):
                dve.wait_ge(ln.sd, n + 1)
                nc.vector.reciprocal(rs[:, n], sd[:, n]).then_inc(ln.rs, 1)
                dve.wait_ge(ln.rs, n + 1)
                dve.wait_ge(ln.var, n + 1)
                nc.vector.tensor_tensor(dst, xc[:, n], rs[:, n].unsqueeze(1).to_broadcast([P, DC, HT]),
                                        ALU.mult).then_inc(ln.out, 1)

            centre(ln1, 0, h0)
            centre(ln1, 1, h0)
            scale(ln1, 0, sq[:, 0])
            scale(ln1, 1, sq[:, 1])
            for n in range(NH):
                for c in range(DC):
                    dve.wait_ge(qk_mm, 4 * n + 2 + c + 1)
                    nc.vector.tensor_scalar(kT[:, c, n * HT:(n + 1) * HT], ps[:, 4 * (1 - n) + 2 + c, 0:HT],
                                            vec[:, C_KB + c:C_KB + c + 1], None, ALU.add).then_inc(k_done, 1)

            def ahead(p, par):
                dve.wait_ge(s_mm, p + 1)
                if not (isinstance(p, int) and p < 2):
                    dve.wait_ge(s_exp, p - 1)
                for c in range(DC):
                    nc.vector.tensor_reduce(
                        mx[0:QROWS, par, c * HC:(c + 1) * HC],
                        ps[0:QROWS, 2 * par + c, 0:HC * S].rearrange("p (h s) -> p h s", h=HC),
                        AX.X, ALU.max).then_inc(s_max, 1)
                dve.wait_ge(s_max, p * 2 + 2)
                for c in range(DC):
                    nc.vector.tensor_tensor(
                        dsc[0:QROWS, par, c * HC:(c + 1) * HC],
                        ps[0:QROWS, 2 * par + c, 0:HC * S].rearrange("p (h s) -> p h s", h=HC),
                        mx[0:QROWS, par, c * HC:(c + 1) * HC].unsqueeze(2).to_broadcast([QROWS, HC, S]),
                        ALU.subtract).then_inc(s_cen, 1)

            def rest(p, par):
                dve.wait_ge(v_mm, p + 1)
                after(dve, pv_mm, p)
                for u in range(2):
                    nc.vector.tensor_tensor(v3[:, u], ps[0:G3 * S, 6, u * D:(u + 1) * D],
                                            cst[0:G3 * S, C_M3:C_M3 + D], ALU.mult).then_inc(v_done, 1)
                dve.wait_ge(s_exp, p + 1)
                nc.vector.tensor_reduce(sm[0:QROWS, par], prob[0:QROWS, par], AX.X, ALU.add).then_inc(s_sum, 1)
                dve.wait_ge(s_sum, p + 1)
                nc.vector.reciprocal(rsm[0:QROWS, par], sm[0:QROWS, par]).then_inc(s_rec, 1)
                dve.wait_ge(s_rec, p + 1)
                dve.wait_ge(pv_mm, p + 1)
                after(dve, ct_mm, p)
                nc.vector.tensor_tensor(
                    cx[0:QROWS], ps[0:QROWS, 7, 0:D].rearrange("p (h d) -> p h d", h=H),
                    rsm[0:QROWS, par].unsqueeze(2).to_broadcast([QROWS, H, DH]), ALU.mult).then_inc(cx_done, 1)

            over_pairs(dve.Fori, ahead, rest)

            for n in range(NH):
                for c in range(DC):
                    dve.wait_ge(op_mm, 2 * n + c + 1)
                    nc.vector.scalar_tensor_tensor(
                        h1[:, c, n * HT:(n + 1) * HT], ps[:, 2 * n + c, 0:HT], vec[:, C_OUTB + c:C_OUTB + c + 1],
                        h0[:, c, n * HT:(n + 1) * HT], ALU.add, ALU.add).then_inc(op_done, 1)
            centre(ln2, 0, h1)
            centre(ln2, 1, h1)
            scale(ln2, 0, sq[:, 0])
            scale(ln2, 1, sq[:, 1])
            for n in range(NH):
                dve.wait_ge(z1_mm, n + 1)
                nc.vector.tensor_copy(z1[:, n], ps[:, n, 0:HT]).then_inc(z1_done, 1)
                dve.wait_ge(z2_mm, n + 1)
                nc.vector.tensor_copy(z2[:, n], ps[:, 4 + n, 0:HT]).then_inc(z2_done, 1)
                dve.wait_ge(sum_done, n + 1)
                for c in range(DC):
                    dve.wait_ge(mo_mm, 2 * n + c + 1)
                    nc.vector.scalar_tensor_tensor(
                        hs[:, c, n * HT:(n + 1) * HT], ps[:, 6 + c, 0:HT], vec[:, C_FC2B + c:C_FC2B + c + 1],
                        hs[:, c, n * HT:(n + 1) * HT], ALU.add, ALU.add).then_inc(mo_done, 1)
            centre(ln3, 0, hs)
            centre(ln3, 1, hs)

            def scale_h3(n):
                dve.wait_ge(ln3.sd, n + 1)
                nc.vector.reciprocal(rs[:, n], sd[:, n]).then_inc(ln3.rs, 1)
                dve.wait_ge(ln3.rs, n + 1)
                nc.vector.tensor_tensor(half(h3, n), xc[:, n], rs[:, n].unsqueeze(1).to_broadcast([P, DC, HT]),
                                        ALU.mult).then_inc(ln3.aff, 1)

            scale_h3(0)
            scale_h3(1)
            for n in range(NH):
                dve.wait_ge(xs_hi, n + 1)
                nc.vector.tensor_tensor(half(x_lo, n), half(h3, n), half(x_hi, n).bitcast(F32),
                                        ALU.subtract).then_inc(xs_lo, 1)

            step = [0]

            def link(ins):
                ins.then_inc(gt, 1)
                step[0] += 1

            def linked():
                dve.wait_ge(gt, step[0])

            dve.wait_ge(lg_mm, 1)
            lps = ps[:, 3, 0:TT * 16].rearrange("p (t e) -> p t e", t=TT)[:, :, 0:E]
            link(nc.vector.tensor_reduce(g1[:, :], lps, AX.X, ALU.max))
            linked()
            link(nc.vector.tensor_tensor(lg[:, :, 0:E], lps, g1[:, :].unsqueeze(2).to_broadcast([P, TT, E]),
                                         ALU.subtract))
            dve.wait_ge(gt_exp, 1)
            link(nc.vector.tensor_reduce(g1[:, :], lg[:, :, 0:E], AX.X, ALU.add))
            linked()
            link(nc.vector.reciprocal(g2[:, :], g1[:, :]))
            linked()
            link(nc.vector.tensor_tensor(lg[:, :, 0:E], lg[:, :, 0:E],
                                         g2[:, :].unsqueeze(2).to_broadcast([P, TT, E]), ALU.mult))
            linked()
            for t in range(TT):
                nc.vector.max(top[:, t], lg[:, t]).then_inc(top_done, 1)
            dve.wait_ge(top_done, TT)
            nc.vector.memset(top[:, :, TOPK:8], -1.0).then_inc(top_done, 1)
            link(nc.vector.tensor_reduce(g1[:, :], top[:, :, 0:TOPK], AX.X, ALU.add))
            linked()
            dve.wait_ge(top_done, TT + 1)
            for t in range(TT):
                nc.vector.match_replace(rep[:, t], top[:, t], lg[:, t], 0.0).then_inc(top_done, 1)
            nc.vector.tensor_scalar(g2[:, :], g1[:, :], 1e-20, None, ALU.add).then_inc(top_done, 1)
            dve.wait_ge(top_done, 2 * TT + 2)
            link(nc.vector.reciprocal(g1[:, :], g2[:, :]))
            nc.vector.tensor_tensor(rep[:, :, 0:E], lg[:, :, 0:E], rep[:, :, 0:E], ALU.subtract) \
                .then_inc(top_done, 1)
            linked()
            dve.wait_ge(top_done, 2 * TT + 3)
            link(nc.vector.tensor_tensor(comb[:, :, NS:NE], rep[:, :, 0:E],
                                         g1[:, :].unsqueeze(2).to_broadcast([P, TT, E]), ALU.mult))
            linked()
            link(nc.vector.transpose(combT[:, :, :].rearrange("p t c -> p (t c)"),
                                     comb[:, :, :].rearrange("p t c -> p (t c)")))
            assert step[0] == GATE_STEPS

            def act_lo(k, u):
                dve.wait_ge(ah_done, k + 1)
                nc.vector.tensor_tensor(a_lo[:, u], t2[:, u % 2], a_hi[:, u].bitcast(F32),
                                        ALU.subtract).then_inc(al_done, 1)

            def expert(e, par, turn):
                for u in range(4):
                    k = e * 4 + u
                    n, j = u // 2, u % 2
                    dve.wait_ge(x_mm, k + 1)
                    dve.wait_ge(gel_done, k + 1)
                    if u == 0:
                        dve.wait_ge(small_done, e + 1)
                    nc.vector.scalar_tensor_tensor(
                        t1[:, j], ps[:, 5 + 2 * j, 0:HT], small[:, par, 2 + j:3 + j], gel[:, j],
                        ALU.add, ALU.mult).then_inc(t1_done, 1)
                    if not (isinstance(k, int) and k == 0):
                        act_lo(k - 1, (u - 1) % 4)
                    dve.wait_ge(t1_done, k + 1)
                    if isinstance(e, int) and e < 2:
                        weight = ones_t[:, :]
                    else:
                        if u == 0:
                            dve.wait_ge(ld_cb[par], 16 * turn)
                        weight = cb[:, par, n * HT:(n + 1) * HT]
                    if not (isinstance(k, int) and k < 2):
                        dve.wait_ge(al_done, k - 1)
                    nc.vector.scalar_tensor_tensor(
                        t2[:, j], t1[:, j], small[:, par, 4 + j:5 + j], weight,
                        ALU.mult, ALU.mult).then_inc(t2_done, 1)

            over_experts(dve.Fori, expert)
            act_lo(4 * NE - 1, 3)
            for n in range(NH):
                for c in range(DC):
                    dve.wait_ge(y_fin, 2 * n + c + 1)
                    nc.vector.tensor_tensor(hs[:, c, n * HT:(n + 1) * HT], ps[:, 2 * n + c, 0:HT],
                                            h3[:, c, n * HT:(n + 1) * HT], ALU.add).then_inc(y_done, 1)
            centre(ln4, 0, hs)
            centre(ln4, 1, hs)
            scale(ln4, 0, sq[:, 0])
            scale(ln4, 1, sq[:, 1])

        @block.tensor
        def _(pe):
            def mean(ln, n, src, wait=None):
                if wait:
                    pe.wait_ge(*wait)
                for c in range(DC):
                    last = mm(ps[:, ln.mean_bank + n, 0:HT], ones_d, src[:, c, n * HT:(n + 1) * HT], c == 0, c == DC - 1)
                last.then_inc(ln.mean, 1)

            def var(ln, n):
                pe.wait_ge(ln.sq, n + 1)
                for c in range(DC):
                    last = mm(ps[:, ln.var_bank + n, 0:HT], ones_d, sq[:, n, c], c == 0, c == DC - 1)
                last.then_inc(ln.var, 1)

            def compose(i):
                pe.wait_ge(ld_qkv[i], 32)
                pe.wait_ge(emb_done, 3 + i)
                for c in range(DC):
                    for j in range(H // 2):
                        last = mm(ps[:, i, c * D + 2 * DH * j:c * D + 2 * DH * (j + 1)],
                                  ut_sb[:, i, j, c * P:(c + 1) * P], vb_sb[:, i, j])
                last.then_inc(cmp_mm, 1)

            pe.wait_ge(psum_clear, 1)
            for n in range(NH):
                for c in range(DC):
                    for k in range(KP):
                        if n == 0 and c == 0:
                            pe.wait_ge(ld_patch[k], 32)
                        last = mm(ps[:, 2 * n + c, 0:HP], tw_sb[:, k, c * P:(c + 1) * P],
                                  pt_sb[:, k, n * HP:(n + 1) * HP], k == 0, k == KP - 1)
                    last.then_inc(emb_mm, 1)
            pe.wait_ge(ld_cst, 16)
            compose(0)
            mean(ln1, 0, h0, (emb_done, 4))
            compose(1)
            mean(ln1, 1, h0, (emb_done, 6))
            var(ln1, 0)
            compose(2)
            var(ln1, 1)
            pe.wait_ge(ld_out, 32)
            for c in range(DC):
                for k in range(2):
                    last = mm(ps[:, 3, c * D:(c + 1) * D], ou_sb[:, k, c * P:(c + 1) * P], ov_sb[:, k], k == 0, k == 1)
            last.then_inc(cmp_mm, 1)
            pe.wait_ge(ln1.sd, 2)
            for n in range(NH):
                pe.wait_ge(ln1.aff, 2 * n + 2)
                pe.wait_ge(cmp_done, 2 + 2 * n)
                for i in range(2):
                    for c in range(DC):
                        for k in range(DC):
                            last = mm(ps[:, 4 * (1 - n) + 2 * i + c, 0:HT], wqkv[:, i, k, c * P:(c + 1) * P],
                                      xn[:, k, n * HT:(n + 1) * HT], k == 0, k == DC - 1)
                        last.then_inc(qk_mm, 1)

            def ahead(p, par):
                if isinstance(p, int) and p == 0:
                    pe.wait_ge(init_done, 6)
                    pe.wait_ge(q_done, 8)
                    pe.wait_ge(k_done, 4)
                pe.wait_ge(staged, 7 * (p + 1))
                if not (isinstance(p, int) and p < 2):
                    pe.wait_ge(s_cen, p * 2 - 2)
                for u in range(2):
                    for c in range(DC):
                        o = ps[QB * u:QB * u + S, 2 * par + c, 0:HC * S]
                        mm(o, qst[:, par, c, u * S:(u + 1) * S],
                           kblk[:, par, u, c].rearrange("p h s -> p (h s)"), True, False)
                        last = mm(o, ident_bf[0:S, :], caus_bf[0:S, :], False, True)
                last.then_inc(s_mm, 1)

            def rest(p, par):
                after(pe, v_done, p * 2)
                for u in range(2):
                    for k in range(DC):
                        last = mm(ps[0:G3 * S, 6, u * D:(u + 1) * D], xst[:, par, k, u], wqkv[:, 2, k], k == 0, k == DC - 1)
                last.then_inc(v_mm, 1)
                pe.wait_ge(s_exp, p + 1)
                after(pe, tr_done, p * 2)
                for g in range(NG):
                    hh = min(G3, H - g * G3)
                    last = nc.tensor.transpose(
                        ps[0:hh * S, 4 + g // G3, (g % G3) * QROWS:(g % G3 + 1) * QROWS],
                        prob[0:QROWS, par, g * G3:g * G3 + hh].rearrange("p h s -> p (h s)"),
                        cst[0:QROWS, C_ID:C_ID + QROWS])
                last.then_inc(tr_mm, 1)
                pe.wait_ge(v_done, p * 2 + 2)
                pe.wait_ge(tr_done, p * 2 + 2)
                after(pe, cx_done, p)
                after(pe, ct_done, p * 2)
                for u in range(2):
                    for g in range(NG):
                        hh = min(G3, H - g * G3)
                        last = mm(ps[QB * u:QB * u + S, 7, g * G3 * DH:(g * G3 + hh) * DH],
                                  pT[0:hh * S, g, QB * u:QB * u + S],
                                  v3[0:hh * S, u, g * G3 * DH:(g * G3 + hh) * DH])
                last.then_inc(pv_mm, 1)
                pe.wait_ge(cx_done, p + 1)
                for c in range(DC):
                    last = nc.tensor.transpose(ps[:, 7, 256 + c * P:256 + c * P + QROWS],
                                               cx[0:QROWS, c * HC:(c + 1) * HC].rearrange("p h d -> p (h d)"),
                                               cst[0:QROWS, C_ID:C_ID + QROWS])
                last.then_inc(ct_mm, 1)

            over_pairs(pe.Fori, ahead, rest)

            pe.wait_ge(ct_done, 2 * PAIRS)
            pe.wait_ge(s_cen, 2 * PAIRS)
            pe.wait_ge(cmp_done, 4)
            for n in range(NH):
                for c in range(DC):
                    for k in range(DC):
                        last = mm(ps[:, 2 * n + c, 0:HT], wo[:, k, c * P:(c + 1) * P],
                                  cT[:, k, n * HT:(n + 1) * HT], k == 0, k == DC - 1)
                    last.then_inc(op_mm, 1)
            mean(ln2, 0, h1, (op_done, 2))
            mean(ln2, 1, h1, (op_done, 4))
            var(ln2, 0)
            var(ln2, 1)
            pe.wait_ge(ld_mlp, 64)
            for n in range(NH):
                pe.wait_ge(ln2.aff, 2 * n + 2)
                for k in range(DC):
                    last = mm(ps[:, n, 0:HT], f1u[:, k], xn[:, k, n * HT:(n + 1) * HT], k == 0, k == DC - 1)
                last.then_inc(z1_mm, 1)
                pe.wait_ge(z1_done, n + 1)
                for f in range(FIC):
                    if n * FIC + f >= 2:
                        pe.wait_ge(hm_done, n * FIC + f - 1)
                    mm(ps[:, 2 + f % 2, 0:HT], f1v[:, f * P:(f + 1) * P], z1[:, n]).then_inc(hm_mm, 1)
                pe.wait_ge(ln2.sd, 2)
                for f in range(FIC):
                    pe.wait_ge(hm_done, n * FIC + f + 1)
                    last = mm(ps[:, 4 + n, 0:HT], f2u[:, f], hm[:, f], f == 0, f == FIC - 1)
                last.then_inc(z2_mm, 1)
                pe.wait_ge(z2_done, n + 1)
                for c in range(DC):
                    if n:
                        pe.wait_ge(mo_done, c + 1)
                    mm(ps[:, 6 + c, 0:HT], f2v[:, c * P:(c + 1) * P], z2[:, n]).then_inc(mo_mm, 1)
            mean(ln3, 0, hs, (mo_done, 2))
            mean(ln3, 1, hs, (mo_done, 4))
            var(ln3, 0)
            var(ln3, 1)
            pe.wait_ge(ln3.aff, 2)
            pe.wait_ge(ld_gate, 16)
            pe.wait_ge(init_done, 6)
            for t in range(TT):
                rows = P if t < TT - 1 else LAST
                for k in range(DC):
                    last = mm(ps[0:rows, 3, 16 * t:16 * t + E], h3[:, k, t * P:t * P + rows], gw[:, k], k == 0, k == DC - 1)
            last.then_inc(lg_mm, 1)

            def down(k, u, par, first=False):
                n, j = u // 2, u % 2
                pe.wait_ge(al_done, k + 1)
                for c in range(DC):
                    last = weight3(lambda w: w[:, par, W1C + j * D + c * P:W1C + j * D + (c + 1) * P],
                                   ps[:, 2 * n + c, 0:HT], w_hi, w_lo, a_hi[:, u], a_lo[:, u],
                                   first, False)
                last.then_inc(y_mm, 1)

            def expert(e, par, turn):
                for u in range(4):
                    k = e * 4 + u
                    n, j = u // 2, u % 2
                    if u == 0:
                        pe.wait_ge(w1_lo_done, e + 1)
                        pe.wait_ge(w2_lo_done, e + 1)
                    if isinstance(e, int) and e == 0 and j == 0:
                        pe.wait_ge(xs_lo, n + 1)
                    if isinstance(k, int) and k == 4 * 0 + 2:
                        pe.wait_ge(gt, 2)
                    if not (isinstance(k, int) and k < 2):
                        pe.wait_ge(t1_done, k - 1)
                    for which, done in ((1, g_mm), (0, x_mm)):
                        for c in range(DC):
                            at = c * 2 * F + which * F + j * P
                            last = weight3(lambda w: w[:, par, at:at + P],
                                           ps[:, 4 + 2 * j + (1 - which), 0:HT], w_hi, w_lo,
                                           x_hi[:, c, n * HT:(n + 1) * HT], x_lo[:, c, n * HT:(n + 1) * HT],
                                           c == 0, c == DC - 1)
                        last.then_inc(done, 1)
                    if u >= 2:
                        down(k - 2, u - 2, par, first=isinstance(e, int) and e == 0 and u == 2)
                    elif not (isinstance(e, int) and e == 0):
                        down(k - 2, u + 2, 1 - par, first=isinstance(e, int) and e == 1 and u == 0)

            over_experts(pe.Fori, expert)
            down(4 * NE - 2, 2, (NE - 1) % 2)
            down(4 * NE - 1, 3, (NE - 1) % 2)
            pe.wait_ge(ld_b2, 16)
            pe.wait_ge(ld_c17, 16)
            for n in range(NH):
                for c in range(DC):
                    mm(ps[:, 2 * n + c, 0:HT], b2_sb[:, c * P:(c + 1) * P],
                       comb17[:, n * HT:(n + 1) * HT], False, True).then_inc(y_fin, 1)
            mean(ln4, 0, hs, (y_done, 2))
            mean(ln4, 1, hs, (y_done, 4))
            var(ln4, 0)
            var(ln4, 1)


def _features(a):
    a = np.asarray(a)
    a = np.moveaxis(a, -1, 0)
    a = a.reshape((a.shape[0] // P, P) + a.shape[1:])
    return np.ascontiguousarray(np.moveaxis(a, 0, 1))


def kernel(**inputs):
    import concourse.bacc as bacc
    from concourse.bass_utils import run_bass_kernel_spmd as run

    a = {k.replace("L0_", ""): np.asarray(v) for k, v in inputs.items()}
    f32 = np.float32
    arrays = {}
    g = IMG // PATCH
    x = a["x"].reshape(B, CH, g, PATCH, g, PATCH).transpose(0, 2, 4, 1, 3, 5).reshape(B * NPATCH, KP * P)
    arrays["patches"] = _features(x)
    arrays["tok_w"] = _features(a["tok_W"])
    cols = [_features(a["tok_b"]), _features(a["tok_pos_embedding"][0]), _features(a["tok_cls_token"][0, 0]),
            _features(a["attn_ln1_g"]), _features(a["attn_ln1_b"]), _features(a["attn_ln2_g"]),
            _features(a["attn_ln2_b"]), _features(a["attn_q_b"].reshape(D)), _features(a["attn_k_b"].reshape(D)),
            _features(a["attn_v_b"].reshape(D)), _features(a["attn_out_b"]), _features(a["attn_fc1_b"]),
            _features(a["attn_fc2_b"])]
    arrays["vecs"] = np.concatenate([c.reshape(P, -1) for c in cols], axis=1)
    p = np.arange(P)[:, None]
    arrays["csts"] = np.concatenate([
        np.eye(P), np.full((P, P), 1.0 / D), (p // DH == np.arange(HC)[None, :]),
        (p // S == (np.arange(D)[None, :] // DH) % G3),
        np.where(np.tile(np.arange(S), HC)[None, :] > p, -1e9, 0.0)], axis=1).astype(f32)
    us, vs = [], []
    for w in "qkv":
        us.append(a[f"attn_{w}_U"].transpose(1, 2, 0).reshape(H // 2, 2 * R, D).transpose(1, 0, 2))
        v = a[f"attn_{w}_V"]
        blk = np.zeros((2 * R, H // 2, 2 * DH), f32)
        for i in range(2):
            blk[i * R:(i + 1) * R, :, i * DH:(i + 1) * DH] = v[i::2].transpose(1, 0, 2)
        vs.append(blk)
    arrays["ut"] = np.stack(us, axis=1)
    arrays["vblk"] = np.stack(vs, axis=1)
    arrays["out_u"] = a["attn_out_U"].T.reshape(2, RO, D).transpose(1, 0, 2)
    arrays["out_v"] = a["attn_out_V"].reshape(2, RO, D).transpose(1, 0, 2)
    arrays["fc1_u"] = a["attn_fc1_U"].reshape(DC, P, R_MLP).transpose(1, 0, 2)
    arrays["fc1_v"] = a["attn_fc1_V"]
    arrays["fc2_u"] = a["attn_fc2_U"].reshape(FIC, P, R_MLP).transpose(1, 0, 2)
    arrays["fc2_v"] = a["attn_fc2_V"]
    arrays["gate"] = _features(a["ffn_gate_w"])
    sw1 = a["ffn_s_fc1_w"].reshape(2, NS, F, D).transpose(1, 0, 2, 3).reshape(NS, 2 * F, D)
    sw2 = a["ffn_s_fc2_w"].reshape(D, NS, F).transpose(1, 0, 2)
    sb1 = a["ffn_s_fc1_b"].reshape(2, NS, F).transpose(1, 0, 2).reshape(NS, 2 * F)
    w1 = np.concatenate([sw1, a["ffn_fc1_w"]])
    w2 = np.concatenate([sw2, a["ffn_fc2_w"]])
    b1 = np.concatenate([sb1, a["ffn_fc1_b"]])
    mult = np.concatenate([a["ffn_s_geglu_mult"].reshape(NS, F), a["ffn_geglu_mult"]])
    packs = []
    for e in range(NE):
        packs.append(np.concatenate([
            w1[e].T.reshape(DC, P, 2 * F).transpose(1, 0, 2).reshape(P, W1C),
            w2[e].T.reshape(F // P, P, D).transpose(1, 0, 2).reshape(P, W2C),
            _features(b1[e][F:]).reshape(P, -1), _features(b1[e][:F]).reshape(P, -1),
            _features(mult[e]).reshape(P, -1)], axis=1))
    arrays["experts"] = np.concatenate(packs)
    arrays["b2"] = np.concatenate([a["ffn_s_fc2_b"][None], np.zeros((NS - 1, D), f32), a["ffn_fc2_b"]])
    arrays = {k: np.ascontiguousarray(v) for k, v in arrays.items()}

    nc = bacc.Bacc("TRN2", target_bir_lowering=False, num_devices=1)
    args = [nc.dram_tensor(k, v.shape, F32, kind="ExternalInput").ap() for k, v in arrays.items()]
    out = nc.dram_tensor("out", (D, T), F32, kind="ExternalOutput").ap()
    comb_dram = nc.dram_tensor("comb_dram", (NE, TPAD), F32, kind="Internal").ap()
    vit_tower_kernel(nc, *args, out, comb_dram)
    r = run(nc, [arrays], core_ids=[0])
    return np.ascontiguousarray(r.results[0]["out"].T.reshape(B, S, D))
```

```python
from contextlib import ExitStack

import numpy as np
import concourse.bass as bass
from concourse import mybir

F32 = mybir.dt.float32
F32R = mybir.dt.float32r
BF16 = mybir.dt.bfloat16
ACT = mybir.ActivationFunctionType
ALU = mybir.AluOpType
AX = mybir.AxisListType

P = 128
B, CH, IMG, PATCH = 16, 3, 96, 16
NPATCH = (IMG // PATCH) ** 2
S = NPATCH + 1
T = B * S
NH = 2
HB = B // NH
HT = T // NH
HP = HB * NPATCH
D = 256
DC = D // P
KP = CH * PATCH * PATCH // P
H, DH, R = 16, 16, 48
HC = P // DH
R_OUT, RO = 192, 96
R_MLP = 128
FI = 4 * D
FIC = FI // P
E, TOPK, F, FS = 15, 3, 256, 512
NS = FS // F
NE = NS + E
W1C, W2C = DC * 2 * F, F // P * D
SMALL = 3 * (F // P)
EXP_COLS = W1C + W2C + SMALL
G3 = 3
NG = (H + G3 - 1) // G3
PAIRS = B // 2
QB = 64
QROWS = QB + S
PSLOT = (0, 1, 2, 4, 5, 3)
TT = 5
LAST = T - (TT - 1) * P
TPAD = TT * P
EPS = 1e-5
GATE_STEPS = 9
LOG_COLS = 20

_v = 0


def _col(n):
    global _v
    _v += n
    return _v - n


C_TOKB, C_POS, C_CLS = _col(DC), _col(DC * S), _col(DC)
C_LN1G, C_LN1B, C_LN2G, C_LN2B = _col(DC), _col(DC), _col(DC), _col(DC)
C_QB, C_KB, C_VB, C_OUTB = _col(DC), _col(DC), _col(DC), _col(DC)
C_FC1B, C_FC2B = _col(FIC), _col(DC)
NVEC = _v
_v = 0
C_ID, C_ONES, C_BLK, C_M3, C_CAUS = _col(P), _col(P), _col(HC), _col(D), _col(HC * S)
NCST = _v


def vit_tower_kernel(nc, patches, tok_w, vecs, csts, ut, vblk, out_u, out_v, fc1_u, fc1_v, fc2_u, fc2_v,
                     gate, experts, b2, out, comb_dram):
    ctx = ExitStack()
    with ctx:
        def sb(name, shape, dt=F32):
            return ctx.enter_context(nc.sbuf_tensor(name, shape, dt))

        def sem(name):
            return ctx.enter_context(nc.semaphore(name))

        pt_mem = sb("patches_sb", [P, KP * B * NPATCH])
        pt_sb = pt_mem[:, :].rearrange("p (k n) -> p k n", k=KP)
        tw_mem = sb("tok_w_sb", [P, KP * D])
        tw_sb = tw_mem[:, :].rearrange("p (k n) -> p k n", k=KP)
        vec = sb("vec_sb", [P, NVEC])
        cst = sb("cst_sb", [P, NCST])
        ident, ones_d = cst[:, C_ID:C_ID + P], cst[:, C_ONES:C_ONES + P]
        eps_t = sb("eps_t", [P, 1])
        warm = sb("warm", [P, 2])
        ident_bf = sb("ident_bf", [P, S], BF16)
        caus_bf = sb("caus_bf", [P, HC * S], BF16)
        h0 = sb("h0", [P, DC, T])
        xn = sb("xn", [P, DC, T])
        qT = sb("qT", [P, DC, T])
        vT = sb("vT", [P, DC, T])
        kT = sb("kT", [P, DC, T])
        h3 = sb("h3", [P, DC, T])
        ut_mem = sb("ut_sb", [P, 3 * H // 2 * D])
        ut_sb = ut_mem[0:2 * R, :].rearrange("p (i j d) -> p i j d", i=3, j=H // 2)
        vb_sb = sb("vb_sb", [2 * R, 3, H // 2, 2 * DH])
        wqkv = sb("wqkv", [P, 3, DC, D])
        ou_sb = sb("ou_sb", [RO, 2, D])
        ov_sb = sb("ov_sb", [RO, 2, D])
        wo = sb("wo", [P, DC, D])
        xc = sb("ln_xc", [P, NH, DC, HT])
        sq = sb("ln_sq", [P, NH, DC, HT])
        sd = sb("ln_sd", [P, NH, HT])
        rs = sb("ln_rs", [P, NH, HT])
        qst = sb("qst", [P, 2, DC, 2 * S])
        vst = sb("vst", [P, 2, DC, 2, G3 * S])
        dsc = sb("dsc", [P, 2, H, S])
        prob = sb("prob", [P, 2, H, S])
        mx = sb("mx", [P, 2, H])
        sm = sb("sm", [P, 2, H])
        rsm = sb("rsm", [P, 2, H])
        pT = sb("pT", [G3 * S, NG, QROWS])
        v3 = sb("v3", [G3 * S, 2, D])
        cx = sb("cx", [P, H, DH])
        f1u = sb("f1u", [P, DC, R_MLP])
        f1v = sb("f1v", [P, FI])
        f2u = sb("f2u", [P, FIC, R_MLP])
        f2v = sb("f2v", [P, D])
        gw = sb("gw", [P, DC, E])
        lg = sb("lg", [P, TT, LOG_COLS])
        top = sb("top", [P, TT, 8])
        rep = sb("rep", [P, TT, LOG_COLS])
        g1 = sb("g1", [P, TT])
        g2 = sb("g2", [P, TT])
        comb = sb("comb", [P, TT, 32])
        combT = sb("combT", [P, TT, 32])
        comb17 = sb("comb17", [NE, T])
        b2_sb = sb("b2_sb", [NE, D])
        x_hi = sb("x_hi", [P, DC, T], F32R)
        x_lo = sb("x_lo", [P, DC, T], F32R)
        stage = sb("stage", [P, 2, EXP_COLS])
        small = sb("small", [P, 2, SMALL])
        w_hi = sb("w_hi", [P, 2, W1C + W2C], F32R)
        w_lo = sb("w_lo", [P, 2, W1C + W2C], F32R)
        cb = sb("cb", [P, 2, T])
        ones_t = sb("ones_t", [P, HT])
        t1 = sb("t1", [P, 2, HT])
        t2 = sb("t2", [P, 2, HT])
        a_hi = sb("a_hi", [P, 4, HT], F32R)
        a_lo = sb("a_lo", [P, 4, HT], F32R)

        at = 2 * 2 * DC * HC * S
        kblk = ut_mem[:, 0:at].rearrange("p (a u c h s) -> p a u c h s", a=2, u=2, c=DC, h=HC)
        cT, h1, hs = (ut_mem[:, at + i * DC * T:at + (i + 1) * DC * T].rearrange("p (c t) -> p c t", c=DC)
                      for i in range(3))
        hm = pt_mem[:, 0:FIC * HT].rearrange("p (f t) -> p f t", f=FIC)
        gel = pt_mem[:, FIC * HT:(FIC + 2) * HT].rearrange("p (j t) -> p j t", j=2)
        z1 = tw_mem[:, 0:T].rearrange("p (n t) -> p n t", n=NH)
        z2 = tw_mem[:, T:2 * T].rearrange("p (n t) -> p n t", n=NH)

        ps = ctx.enter_context(nc.psum_tensor("ps", [P, 8, 512], F32))

        ld_patch = [sem(f"ld_patch{k}") for k in range(KP)]
        ld_cst, ld_vec, ld_out = sem("ld_cst"), sem("ld_vec"), sem("ld_out_w")
        ld_qkv = [sem(f"ld_qkv{i}") for i in range(3)]
        ld_mlp, ld_gate, ld_b2 = sem("ld_mlp"), sem("ld_gate"), sem("ld_b2")
        ld_exp = [sem("ld_exp0"), sem("ld_exp1")]
        ld_cb = [sem("ld_cb0"), sem("ld_cb1")]
        ld_c17 = sem("ld_c17")
        st_comb, st_out = sem("st_comb"), sem("st_out")
        init_done, warmed = sem("init_done"), sem("warmed")
        emb_mm, emb_done = sem("emb_mm"), sem("emb_done")
        cmp_mm, cmp_done = sem("cmp_mm"), sem("cmp_done")
        pr_mm, q_done, k_done, vt_done = sem("proj_mm"), sem("q_done"), sem("k_done"), sem("vt_done")
        staged, v_staged = sem("staged"), sem("v_staged")
        s_mm, s_max, s_cen, s_exp, s_sum, s_rec = (sem(n) for n in ("s_mm", "s_max", "s_cen", "s_exp", "s_sum", "s_rec"))
        v_mm, v_done, tr_mm, tr_done = sem("v_mm"), sem("v_done"), sem("tr_mm"), sem("tr_done")
        pv_mm, cx_done, ct_mm, ct_done = sem("pv_mm"), sem("cx_done"), sem("ct_mm"), sem("ct_done")
        op_mm, op_done = sem("op_mm"), sem("op_done")
        sum_done = sem("sum_done")
        z1_mm, z1_done, hm_mm, hm_done = sem("z1_mm"), sem("z1_done"), sem("hm_mm"), sem("hm_done")
        z2_mm, z2_done, mo_mm, mo_done = sem("z2_mm"), sem("z2_done"), sem("mo_mm"), sem("mo_done")
        lg_mm, gt, top_done = sem("lg_mm"), sem("gate_chain"), sem("top_done")
        gt_exp = sem("gate_exp")
        xs_hi, xs_lo = sem("xs_hi"), sem("xs_lo")
        w1_hi_done, w2_hi_done, w1_lo_done, w2_lo_done = sem("w1_hi"), sem("w2_hi"), sem("w1_lo"), sem("w2_lo")
        small_done = sem("small_done")
        g_mm, x_mm, gel_done, t1_done, t2_done = sem("g_mm"), sem("x_mm"), sem("gel_done"), sem("t1_done"), sem("t2_done")
        ah_done, al_done, y_mm = sem("ah_done"), sem("al_done"), sem("y_mm")
        y_fin, y_done = sem("y_fin"), sem("y_done")

        class Norm:

            def __init__(self, name, mean_bank, var_bank):
                self.mean_bank, self.var_bank = mean_bank, var_bank
                self.mean, self.cen, self.sq = sem(name + "_mean"), sem(name + "_cen"), sem(name + "_sq")
                self.var, self.sd, self.rs = sem(name + "_var"), sem(name + "_sd"), sem(name + "_rs")
                self.out, self.aff = sem(name + "_out"), sem(name + "_aff")

        ln1, ln2, ln3, ln4 = Norm("ln1", 4, 6), Norm("ln2", 4, 6), Norm("ln3", 0, 4), Norm("ln4", 4, 6)

        def half(t, n):
            return t[:, :, n * HT:(n + 1) * HT]

        def mm(o, w, x, start=True, stop=True):
            return nc.tensor.matmul(o, w, x, start=start, stop=stop)

        def weight3(w, o, w_h, w_l, x_h, x_l, first, last):
            mm(o, w(w_h), x_h, start=first, stop=False)
            mm(o, w(w_h), x_l, start=False, stop=False)
            return mm(o, w(w_l), x_h, start=False, stop=last)

        def over_pairs(fori, turn):
            turn(0, 0, True)
            with fori(0, 2) as i:
                turn(i * 2 + 1, 1, True)
                turn(i * 2 + 2, 0, True)
            turn(5, 1, True)
            turn(6, 0, False)
            turn(7, 1, False)

        def after(eng, semaphore, count):
            if not (isinstance(count, int) and count == 0):
                eng.wait_ge(semaphore, count)

        def over_experts(fori, expert):
            expert(0, 0, 0)
            expert(1, 1, 0)
            with fori(0, (NE - 3) // 2) as i:
                expert(i * 2 + 2, 0, i + 1)
                expert(i * 2 + 3, 1, i + 1)
            expert(NE - 1, 0, (NE - 1) // 2)

        def proj_bank(i):
            return (4 + i) % 8

        block = ctx.enter_context(nc.Block())

        @block.sync
        def _(sp):
            for k in range(KP):
                sp.dma_start(tw_sb[:, k], tok_w[:, k]).then_inc(ld_patch[k], 16)
                sp.dma_start(pt_sb[:, k], patches[:, k]).then_inc(ld_patch[k], 16)
            sp.dma_start(vec[:, :], vecs).then_inc(ld_vec, 16)
            sp.dma_start(cst[:, :], csts).then_inc(ld_cst, 16)
            for i in range(3):
                sp.dma_start(ut_sb[:, i], ut[:, i]).then_inc(ld_qkv[i], 16)
                sp.dma_start(vb_sb[:, i], vblk[:, i]).then_inc(ld_qkv[i], 16)
            sp.dma_start(ou_sb[:, :], out_u).then_inc(ld_out, 16)
            sp.dma_start(ov_sb[:, :], out_v).then_inc(ld_out, 16)
            sp.dma_start(f1u[:, :], fc1_u).then_inc(ld_mlp, 16)
            sp.dma_start(f1v[:, :], fc1_v).then_inc(ld_mlp, 16)
            sp.dma_start(f2u[:, :], fc2_u).then_inc(ld_mlp, 16)
            sp.dma_start(f2v[:, :], fc2_v).then_inc(ld_mlp, 16)
            sp.dma_start(gw[:, :], gate).then_inc(ld_gate, 16)
            sp.dma_start(b2_sb[:, :], b2).then_inc(ld_b2, 16)

            def expert(e, par, turn):
                if not (isinstance(e, int) and e < 2):
                    sp.wait_ge(small_done, e - 1)
                sp.dma_start(stage[:, par], experts[bass.ds(e * P, P), :]).then_inc(ld_exp[par], 16)
                if isinstance(e, int) and e == 1:
                    sp.wait_ge(gt, GATE_STEPS)
                    for q in range(4):
                        rows = comb_dram.rearrange("e (t q c) -> e t q c", q=4, c=32)[:, :, q, :]
                        sp.dma_start(rows, combT[32 * q:32 * q + NE, :, :]).then_inc(st_comb, 16)
                    sp.wait_ge(st_comb, 64)
                    sp.dma_start(comb17[:, :], comb_dram[:, 0:T]).then_inc(ld_c17, 16)
                if not (isinstance(e, int) and e < 2):
                    sp.wait_ge(t2_done, 4 * (e - 1))
                    sp.dma_start(cb[:, par], comb_dram[bass.ds(e, 1), 0:T].to_broadcast([P, T])) \
                        .then_inc(ld_cb[par], 16)

            over_experts(sp.Fori, expert)

            for n in range(NH):
                sp.wait_ge(ln4.out, n + 1)
                for c in range(DC):
                    sp.dma_start(out[c * P:(c + 1) * P, n * HT:(n + 1) * HT], sq[:, n, c]).then_inc(st_out, 16)
            sp.wait_ge(st_out, 16 * NH * DC)

        @block.gpsimd
        def _(pool):
            def stage_pair(p, par):
                if not (isinstance(p, int) and p < 2):
                    pool.wait_ge(s_mm, p - 1)
                t0 = p * (2 * S)
                for u in range(2):
                    for c in range(DC):
                        pool.tensor_tensor(
                            kblk[:, par, u, c],
                            kT[:, c, bass.ds(t0 + u * S, S)].unsqueeze(1).to_broadcast([P, HC, S]),
                            cst[:, C_BLK:C_BLK + HC].unsqueeze(2).to_broadcast([P, HC, S]),
                            ALU.mult).then_inc(staged, 1)
                pool.tensor_copy(qst[:, par], qT[:, :, bass.ds(t0, 2 * S)]).then_inc(staged, 1)

            pool.wait_ge(q_done, 2)
            pool.wait_ge(k_done, 2)
            stage_pair(0, 0)
            stage_pair(1, 1)
            pool.wait_ge(q_done, 4)
            pool.wait_ge(k_done, 4)
            over_pairs(pool.Fori, lambda p, par, more: stage_pair(p + 2, par) if more else None)

            for n in range(NH):
                pool.wait_ge(op_done, DC * (n + 1))
                pool.tensor_tensor(half(hs, n), half(h0, n), half(h1, n), ALU.add).then_inc(sum_done, 1)

            def split_lo(e, par, turn):
                pool.wait_ge(w1_hi_done, e + 1)
                if not (isinstance(e, int) and e < 2):
                    pool.wait_ge(x_mm, 4 * (e - 1))
                pool.tensor_tensor(w_lo[:, par, 0:W1C], stage[:, par, 0:W1C],
                                   w_hi[:, par, 0:W1C].bitcast(F32), ALU.subtract).then_inc(w1_lo_done, 1)
                pool.wait_ge(w2_hi_done, e + 1)
                if not (isinstance(e, int) and e < 2):
                    pool.wait_ge(y_mm, 4 * (e - 1))
                pool.tensor_tensor(w_lo[:, par, W1C:W1C + W2C], stage[:, par, W1C:W1C + W2C],
                                   w_hi[:, par, W1C:W1C + W2C].bitcast(F32), ALU.subtract).then_inc(w2_lo_done, 1)
                pool.tensor_copy(small[:, par], stage[:, par, W1C + W2C:EXP_COLS]).then_inc(small_done, 1)

            over_experts(pool.Fori, split_lo)

        @block.scalar
        def _(act):
            def norm_act(ln, n):
                act.wait_ge(ln.cen, n + 1)
                nc.scalar.activation(sq[:, n], xc[:, n], ACT.Square).then_inc(ln.sq, 1)
                act.wait_ge(ln.var, n + 1)
                nc.scalar.activation(sd[:, n], ps[:, ln.var_bank + n, 0:HT], ACT.Sqrt,
                                     bias=eps_t[:, 0:1]).then_inc(ln.sd, 1)

            def affine_act(ln, n, gamma, beta):
                act.wait_ge(ln.out, n + 1)
                for c in range(DC):
                    nc.scalar.activation(xn[:, c, n * HT:(n + 1) * HT], sq[:, n, c], ACT.Identity,
                                         bias=vec[:, beta + c:beta + c + 1],
                                         scale=vec[:, gamma + c:gamma + c + 1]).then_inc(ln.aff, 1)

            act.wait_ge(ld_vec, 16)
            act.wait_ge(init_done, 2)
            norm_act(ln1, 0)
            norm_act(ln1, 1)
            for i in range(4):
                act.wait_ge(cmp_mm, i + 1)
                nc.scalar.activation(wqkv[:, i].rearrange("p c d -> p (c d)") if i < 3
                                     else wo[:, :].rearrange("p c d -> p (c d)"),
                                     ps[:, i, :], ACT.Copy).then_inc(cmp_done, 1)
            affine_act(ln1, 0, C_LN1G, C_LN1B)
            affine_act(ln1, 1, C_LN1G, C_LN1B)
            for n in range(NH):
                for i, (dst, bias, done) in ((0, (qT, C_QB, q_done)), (2, (vT, C_VB, vt_done))):
                    for c in range(DC):
                        g = 6 * n + 2 * i + c
                        act.wait_ge(pr_mm, g + 1)
                        nc.scalar.activation(dst[:, c, n * HT:(n + 1) * HT], ps[:, proj_bank(g), 0:HT],
                                             ACT.Identity, bias=vec[:, bias + c:bias + c + 1]).then_inc(done, 1)

            def stage_values(p, par):
                for c in range(DC):
                    nc.scalar.activation(
                        vst[:, par, c].rearrange("p u (r s) -> p u r s", r=G3),
                        vT[:, c, bass.ds(p * (2 * S), 2 * S)].rearrange("p (u s) -> p u s", u=2).unsqueeze(2)
                        .to_broadcast([P, 2, G3, S]), ACT.Copy).then_inc(v_staged, 1)

            def exps(p, par):
                act.wait_ge(s_cen, p + 1)
                if not (isinstance(p, int) and p < 2):
                    act.wait_ge(tr_mm, p - 1)
                    act.wait_ge(s_sum, p - 1)
                nc.scalar.activation(prob[0:QROWS, par], dsc[0:QROWS, par], ACT.Exp,
                                     scale=DH ** -0.5).then_inc(s_exp, 1)

            def context_out(p):
                act.wait_ge(ct_mm, p + 1)
                nc.scalar.activation(
                    cT[:, :, bass.ds(p * (2 * S), 2 * S)].rearrange("p c (u s) -> p c u s", u=2),
                    ps[:, 7, 256:256 + DC * P].rearrange("p (c u s) -> p c u s", c=DC, u=2)[:, :, :, 0:S],
                    ACT.Copy).then_inc(ct_done, 1)

            act.wait_ge(vt_done, 2)
            stage_values(0, 0)
            stage_values(1, 1)
            exps(0, 0)
            exps(1, 1)
            act.wait_ge(vt_done, 4)

            def turn(p, par, more):
                act.wait_ge(tr_mm, p + 1)
                after(act, pv_mm, p)
                for k in range(2):
                    nc.scalar.activation(pT[:, k * G3:(k + 1) * G3].rearrange("p g q -> p (g q)"),
                                         ps[0:G3 * S, 4 + k, 0:G3 * QROWS], ACT.Copy).then_inc(tr_done, 1)
                if more:
                    act.wait_ge(v_mm, p + 1)
                    stage_values(p + 2, par)
                if not (isinstance(p, int) and p == 0):
                    context_out(p - 1)
                if more:
                    exps(p + 2, par)

            over_pairs(act.Fori, turn)
            context_out(PAIRS - 1)
            nc.scalar.activation(warm[:, 0:1], eps_t[:, 0:1], ACT.Sqrt).then_inc(warmed, 1)

            norm_act(ln2, 0)
            norm_act(ln2, 1)
            affine_act(ln2, 0, C_LN2G, C_LN2B)
            affine_act(ln2, 1, C_LN2G, C_LN2B)
            for n in range(NH):
                for f in range(FIC):
                    act.wait_ge(hm_mm, FIC * n + f + 1)
                    if n == 1 and f == 0:
                        act.wait_ge(z2_mm, 1)
                    nc.scalar.activation(hm[:, f], ps[:, 2 + f % 2, 0:HT], ACT.Gelu_apprx_tanh,
                                         bias=vec[:, C_FC1B + f:C_FC1B + f + 1]).then_inc(hm_done, 1)
            norm_act(ln3, 0)
            norm_act(ln3, 1)
            for n in range(NH):
                act.wait_ge(ln3.aff, n + 1)
                nc.scalar.activation(half(x_hi, n), half(h3, n), ACT.Copy).then_inc(xs_hi, 1)

            def w1_hi(e, par, turn):
                act.wait_ge(ld_exp[par], 16 * (turn + 1))
                if not (isinstance(e, int) and e < 2):
                    act.wait_ge(x_mm, 4 * (e - 1))
                nc.scalar.activation(w_hi[:, par, 0:W1C], stage[:, par, 0:W1C], ACT.Copy).then_inc(w1_hi_done, 1)

            def w2_hi(e, par, turn):
                if not (isinstance(e, int) and e < 2):
                    act.wait_ge(y_mm, 4 * (e - 1))
                nc.scalar.activation(w_hi[:, par, W1C:W1C + W2C], stage[:, par, W1C:W1C + W2C],
                                     ACT.Copy).then_inc(w2_hi_done, 1)

            w1_hi(0, 0, 0)
            w2_hi(0, 0, 0)
            w1_hi(1, 1, 0)
            w2_hi(1, 1, 0)
            act.wait_ge(gt, 2)
            nc.scalar.activation(lg[:, :, 0:E], lg[:, :, 0:E], ACT.Exp).then_inc(gt_exp, 1)

            def act_hi(k, u):
                act.wait_ge(t2_done, k + 1)
                if not (isinstance(k, int) and k < 4):
                    act.wait_ge(y_mm, k - 3)
                nc.scalar.activation(a_hi[:, u], t2[:, u % 2], ACT.Copy).then_inc(ah_done, 1)

            def expert(e, par, turn):
                for u in range(4):
                    k = e * 4 + u
                    j = u % 2
                    act.wait_ge(g_mm, k + 1)
                    if not (isinstance(k, int) and k < 2):
                        act.wait_ge(t1_done, k - 1)
                    if u == 0:
                        act.wait_ge(small_done, e + 1)
                    nc.scalar.activation(gel[:, u % 2], ps[:, 4 + 2 * (u % 2), 0:HT], ACT.Gelu,
                                         bias=small[:, par, j:j + 1]).then_inc(gel_done, 1)
                    if not (isinstance(k, int) and k == 0):
                        act_hi(k - 1, (u - 1) % 4)
                    more = not (isinstance(e, int) and (e == 0 or e == NE - 1))
                    if u == 0 and more:
                        w1_hi(e + 1, 1 - par, turn + par)
                    if u == 2 and more:
                        w2_hi(e + 1, 1 - par, turn + par)

            over_experts(act.Fori, expert)
            act_hi(4 * NE - 1, 3)
            norm_act(ln4, 0)
            norm_act(ln4, 1)

        @block.vector
        def _(dve):
            nc.vector.memset(eps_t[:, :], EPS).then_inc(init_done, 1)
            nc.vector.memset(ones_t[:, :], 1.0).then_inc(init_done, 1)
            nc.vector.memset(comb[:, :, :], 1.0).then_inc(init_done, 1)
            nc.vector.memset(lg[:, :, :], -1.0).then_inc(init_done, 1)
            dve.wait_ge(ld_cst, 16)
            nc.vector.tensor_copy(ident_bf[:, :], cst[:, C_ID:C_ID + S]).then_inc(init_done, 1)
            nc.vector.tensor_copy(caus_bf[:, :], cst[:, C_CAUS:C_CAUS + HC * S]).then_inc(init_done, 1)
            dve.wait_ge(ld_vec, 16)
            pos = vec[:, C_POS:C_POS + DC * S].rearrange("p (c s) -> p c s", c=DC)
            for c in range(DC):
                hv = h0[:, c, :].rearrange("p (b s) -> p b s", b=B)
                nc.vector.tensor_scalar(hv[:, :, 0], pos[:, c, 0:1].to_broadcast([P, B]),
                                        vec[:, C_CLS + c:C_CLS + c + 1], None, ALU.add).then_inc(emb_done, 1)
            for n in range(NH):
                for c in range(DC):
                    dve.wait_ge(emb_mm, 2 * n + c + 1)
                    hv = h0[:, c, :].rearrange("p (b s) -> p b s", b=B)
                    nc.vector.scalar_tensor_tensor(
                        hv[:, n * HB:(n + 1) * HB, 1:S],
                        ps[:, 2 * n + c, 0:HP].rearrange("p (b s) -> p b s", b=HB),
                        vec[:, C_TOKB + c:C_TOKB + c + 1],
                        pos[:, c, 1:S].unsqueeze(1).to_broadcast([P, HB, NPATCH]),
                        ALU.add, ALU.add).then_inc(emb_done, 1)

            def centre(ln, n, src):
                dve.wait_ge(ln.mean, n + 1)
                nc.vector.tensor_tensor(
                    xc[:, n], half(src, n),
                    ps[:, ln.mean_bank + n, 0:HT].unsqueeze(1).to_broadcast([P, DC, HT]),
                    ALU.subtract).then_inc(ln.cen, 1)

            def scale(ln, n, dst):
                dve.wait_ge(ln.sd, n + 1)
                nc.vector.reciprocal(rs[:, n], sd[:, n]).then_inc(ln.rs, 1)
                dve.wait_ge(ln.rs, n + 1)
                dve.wait_ge(ln.var, n + 1)
                nc.vector.tensor_tensor(dst, xc[:, n], rs[:, n].unsqueeze(1).to_broadcast([P, DC, HT]),
                                        ALU.mult).then_inc(ln.out, 1)

            centre(ln1, 0, h0)
            centre(ln1, 1, h0)
            scale(ln1, 0, sq[:, 0])
            scale(ln1, 1, sq[:, 1])
            for n in range(NH):
                for c in range(DC):
                    g = 6 * n + 2 + c
                    dve.wait_ge(pr_mm, g + 1)
                    nc.vector.tensor_scalar(kT[:, c, n * HT:(n + 1) * HT], ps[:, proj_bank(g), 0:HT],
                                            vec[:, C_KB + c:C_KB + c + 1], None, ALU.add).then_inc(k_done, 1)

            def by_head(par):
                return ps[0:QROWS, 2 * par:2 * par + 2, 0:HC * S].rearrange("p c (h s) -> p c h s", h=HC)

            def maxima(p, par):
                dve.wait_ge(s_mm, p + 1)
                nc.vector.tensor_reduce(mx[0:QROWS, par].rearrange("p (c h) -> p c h", c=DC), by_head(par),
                                        AX.X, ALU.max).then_inc(s_max, 1)

            def centred(p, par):
                if not (isinstance(p, int) and p < 2):
                    dve.wait_ge(s_exp, p - 1)
                dve.wait_ge(s_max, p + 1)
                nc.vector.tensor_tensor(
                    dsc[0:QROWS, par].rearrange("p (c h) s -> p c h s", c=DC), by_head(par),
                    mx[0:QROWS, par].rearrange("p (c h) -> p c h", c=DC).unsqueeze(3)
                    .to_broadcast([QROWS, DC, HC, S]), ALU.subtract).then_inc(s_cen, 1)

            def sums(p, par):
                dve.wait_ge(s_exp, p + 1)
                nc.vector.tensor_reduce(sm[0:QROWS, par], prob[0:QROWS, par], AX.X, ALU.add).then_inc(s_sum, 1)
                dve.wait_ge(s_sum, p + 1)
                nc.vector.reciprocal(rsm[0:QROWS, par], sm[0:QROWS, par]).then_inc(s_rec, 1)

            for p in range(2):
                maxima(p, p)
                centred(p, p)
            sums(0, 0)

            def turn(p, par, more):
                dve.wait_ge(v_mm, p + 1)
                after(dve, pv_mm, p)
                nc.vector.tensor_tensor(
                    v3[:, :], ps[0:G3 * S, 6, :].rearrange("p (u d) -> p u d", u=2),
                    cst[0:G3 * S, C_M3:C_M3 + D].unsqueeze(1).to_broadcast([G3 * S, 2, D]),
                    ALU.mult).then_inc(v_done, 1)
                if not (isinstance(p, int) and p == PAIRS - 1):
                    sums(p + 1, 1 - par)
                if more:
                    maxima(p + 2, par)
                dve.wait_ge(s_rec, p + 1)
                dve.wait_ge(pv_mm, p + 1)
                after(dve, ct_mm, p)
                nc.vector.tensor_tensor(
                    cx[0:QROWS], ps[0:QROWS, 7, 0:D].rearrange("p (h d) -> p h d", h=H),
                    rsm[0:QROWS, par].unsqueeze(2).to_broadcast([QROWS, H, DH]), ALU.mult).then_inc(cx_done, 1)
                if more:
                    centred(p + 2, par)

            over_pairs(dve.Fori, turn)

            for n in range(NH):
                for c in range(DC):
                    dve.wait_ge(op_mm, 2 * n + c + 1)
                    nc.vector.scalar_tensor_tensor(
                        h1[:, c, n * HT:(n + 1) * HT], ps[:, 2 * n + c, 0:HT], vec[:, C_OUTB + c:C_OUTB + c + 1],
                        h0[:, c, n * HT:(n + 1) * HT], ALU.add, ALU.add).then_inc(op_done, 1)
            centre(ln2, 0, h1)
            centre(ln2, 1, h1)
            scale(ln2, 0, sq[:, 0])
            scale(ln2, 1, sq[:, 1])
            for n in range(NH):
                dve.wait_ge(z1_mm, n + 1)
                nc.vector.tensor_copy(z1[:, n], ps[:, n, 0:HT]).then_inc(z1_done, 1)
                dve.wait_ge(z2_mm, n + 1)
                nc.vector.tensor_copy(z2[:, n], ps[:, 4 + n, 0:HT]).then_inc(z2_done, 1)
                dve.wait_ge(sum_done, n + 1)
                for c in range(DC):
                    dve.wait_ge(mo_mm, 2 * n + c + 1)
                    nc.vector.scalar_tensor_tensor(
                        hs[:, c, n * HT:(n + 1) * HT], ps[:, 6 + c, 0:HT], vec[:, C_FC2B + c:C_FC2B + c + 1],
                        hs[:, c, n * HT:(n + 1) * HT], ALU.add, ALU.add).then_inc(mo_done, 1)
            centre(ln3, 0, hs)
            centre(ln3, 1, hs)

            def scale_h3(n):
                dve.wait_ge(ln3.sd, n + 1)
                nc.vector.reciprocal(rs[:, n], sd[:, n]).then_inc(ln3.rs, 1)
                dve.wait_ge(ln3.rs, n + 1)
                nc.vector.tensor_tensor(half(h3, n), xc[:, n], rs[:, n].unsqueeze(1).to_broadcast([P, DC, HT]),
                                        ALU.mult).then_inc(ln3.aff, 1)

            scale_h3(0)
            scale_h3(1)
            for n in range(NH):
                dve.wait_ge(xs_hi, n + 1)
                nc.vector.tensor_tensor(half(x_lo, n), half(h3, n), half(x_hi, n).bitcast(F32),
                                        ALU.subtract).then_inc(xs_lo, 1)

            step = [0]

            def link(ins):
                ins.then_inc(gt, 1)
                step[0] += 1

            def linked():
                dve.wait_ge(gt, step[0])

            dve.wait_ge(lg_mm, 1)
            lps = ps[:, 3, 0:TT * 16].rearrange("p (t e) -> p t e", t=TT)[:, :, 0:E]
            link(nc.vector.tensor_reduce(g1[:, :], lps, AX.X, ALU.max))
            linked()
            link(nc.vector.tensor_tensor(lg[:, :, 0:E], lps, g1[:, :].unsqueeze(2).to_broadcast([P, TT, E]),
                                         ALU.subtract))
            dve.wait_ge(gt_exp, 1)
            link(nc.vector.tensor_reduce(g1[:, :], lg[:, :, 0:E], AX.X, ALU.add))
            linked()
            link(nc.vector.reciprocal(g2[:, :], g1[:, :]))
            linked()
            link(nc.vector.tensor_tensor(lg[:, :, 0:E], lg[:, :, 0:E],
                                         g2[:, :].unsqueeze(2).to_broadcast([P, TT, E]), ALU.mult))
            linked()
            for t in range(TT):
                nc.vector.max(top[:, t], lg[:, t]).then_inc(top_done, 1)
            dve.wait_ge(top_done, TT)
            nc.vector.memset(top[:, :, TOPK:8], -1.0).then_inc(top_done, 1)
            link(nc.vector.tensor_reduce(g1[:, :], top[:, :, 0:TOPK], AX.X, ALU.add))
            linked()
            dve.wait_ge(top_done, TT + 1)
            for t in range(TT):
                nc.vector.match_replace(rep[:, t], top[:, t], lg[:, t], 0.0).then_inc(top_done, 1)
            nc.vector.tensor_scalar(g2[:, :], g1[:, :], 1e-20, None, ALU.add).then_inc(top_done, 1)
            dve.wait_ge(top_done, 2 * TT + 2)
            link(nc.vector.reciprocal(g1[:, :], g2[:, :]))
            nc.vector.tensor_tensor(rep[:, :, 0:E], lg[:, :, 0:E], rep[:, :, 0:E], ALU.subtract) \
                .then_inc(top_done, 1)
            linked()
            dve.wait_ge(top_done, 2 * TT + 3)
            link(nc.vector.tensor_tensor(comb[:, :, NS:NE], rep[:, :, 0:E],
                                         g1[:, :].unsqueeze(2).to_broadcast([P, TT, E]), ALU.mult))
            linked()
            link(nc.vector.transpose(combT[:, :, :].rearrange("p t c -> p (t c)"),
                                     comb[:, :, :].rearrange("p t c -> p (t c)")))
            assert step[0] == GATE_STEPS

            def act_lo(k, u):
                dve.wait_ge(ah_done, k + 1)
                nc.vector.tensor_tensor(a_lo[:, u], t2[:, u % 2], a_hi[:, u].bitcast(F32),
                                        ALU.subtract).then_inc(al_done, 1)

            def expert(e, par, turn):
                for u in range(4):
                    k = e * 4 + u
                    n, j = u // 2, u % 2
                    dve.wait_ge(x_mm, k + 1)
                    dve.wait_ge(gel_done, k + 1)
                    if u == 0:
                        dve.wait_ge(small_done, e + 1)
                    nc.vector.scalar_tensor_tensor(
                        t1[:, j], ps[:, 5 + 2 * j, 0:HT], small[:, par, 2 + j:3 + j], gel[:, j],
                        ALU.add, ALU.mult).then_inc(t1_done, 1)
                    if not (isinstance(k, int) and k == 0):
                        act_lo(k - 1, (u - 1) % 4)
                    dve.wait_ge(t1_done, k + 1)
                    if isinstance(e, int) and e < 2:
                        weight = ones_t[:, :]
                    else:
                        if u == 0:
                            dve.wait_ge(ld_cb[par], 16 * turn)
                        weight = cb[:, par, n * HT:(n + 1) * HT]
                    if not (isinstance(k, int) and k < 2):
                        dve.wait_ge(al_done, k - 1)
                    nc.vector.scalar_tensor_tensor(
                        t2[:, j], t1[:, j], small[:, par, 4 + j:5 + j], weight,
                        ALU.mult, ALU.mult).then_inc(t2_done, 1)

            over_experts(dve.Fori, expert)
            act_lo(4 * NE - 1, 3)
            for n in range(NH):
                for c in range(DC):
                    dve.wait_ge(y_fin, 2 * n + c + 1)
                    nc.vector.tensor_tensor(hs[:, c, n * HT:(n + 1) * HT], ps[:, 2 * n + c, 0:HT],
                                            h3[:, c, n * HT:(n + 1) * HT], ALU.add).then_inc(y_done, 1)
            centre(ln4, 0, hs)
            centre(ln4, 1, hs)
            scale(ln4, 0, sq[:, 0])
            scale(ln4, 1, sq[:, 1])

        @block.tensor
        def _(pe):
            def mean(ln, n, src, wait=None):
                if wait:
                    pe.wait_ge(*wait)
                for c in range(DC):
                    last = mm(ps[:, ln.mean_bank + n, 0:HT], ones_d, src[:, c, n * HT:(n + 1) * HT], c == 0, c == DC - 1)
                last.then_inc(ln.mean, 1)

            def var(ln, n):
                pe.wait_ge(ln.sq, n + 1)
                for c in range(DC):
                    last = mm(ps[:, ln.var_bank + n, 0:HT], ones_d, sq[:, n, c], c == 0, c == DC - 1)
                last.then_inc(ln.var, 1)

            def compose(i):
                pe.wait_ge(ld_qkv[i], 32)
                pe.wait_ge(emb_done, 3 + i)
                for c in range(DC):
                    for j in range(H // 2):
                        last = mm(ps[:, i, c * D + 2 * DH * j:c * D + 2 * DH * (j + 1)],
                                  ut_sb[:, i, j, c * P:(c + 1) * P], vb_sb[:, i, j])
                last.then_inc(cmp_mm, 1)

            for k in range(KP):
                pe.wait_ge(ld_patch[k], 32)
                for n in range(NH):
                    for c in range(DC):
                        last = mm(ps[:, 2 * n + c, 0:HP], tw_sb[:, k, c * P:(c + 1) * P],
                                  pt_sb[:, k, n * HP:(n + 1) * HP], k == 0, k == KP - 1)
                        if k == KP - 1:
                            last.then_inc(emb_mm, 1)
            pe.wait_ge(ld_cst, 16)
            mean(ln1, 0, h0, (emb_done, 4))
            mean(ln1, 1, h0, (emb_done, 6))
            compose(0)
            var(ln1, 0)
            var(ln1, 1)
            compose(1)
            compose(2)
            pe.wait_ge(ld_out, 32)
            for c in range(DC):
                for k in range(2):
                    last = mm(ps[:, 3, c * D:(c + 1) * D], ou_sb[:, k, c * P:(c + 1) * P], ov_sb[:, k], k == 0, k == 1)
            last.then_inc(cmp_mm, 1)
            pe.wait_ge(ln1.sd, 2)
            pe.wait_ge(cmp_done, 3)
            for n in range(NH):
                pe.wait_ge(ln1.aff, 2 * n + 2)
                for i in range(3):
                    for c in range(DC):
                        g = 6 * n + 2 * i + c
                        if g == 4:
                            pe.wait_ge(cmp_done, 4)
                        if g == 8:
                            pe.wait_ge(q_done, 2)
                            pe.wait_ge(k_done, 2)
                        for k in range(DC):
                            last = mm(ps[:, proj_bank(g), 0:HT], wqkv[:, i, k, c * P:(c + 1) * P],
                                      xn[:, k, n * HT:(n + 1) * HT], k == 0, k == DC - 1)
                        last.then_inc(pr_mm, 1)

            def scores(p, par):
                pe.wait_ge(staged, p * 5 + 5)
                if not (isinstance(p, int) and p < 2):
                    pe.wait_ge(s_cen, p - 1)
                for u in range(2):
                    for c in range(DC):
                        o = ps[QB * u:QB * u + S, 2 * par + c, 0:HC * S]
                        mm(o, qst[:, par, c, u * S:(u + 1) * S],
                           kblk[:, par, u, c].rearrange("p h s -> p (h s)"), True, False)
                        last = mm(o, ident_bf[0:S, :], caus_bf[0:S, :], False, True)
                last.then_inc(s_mm, 1)

            def context_transposed(p):
                pe.wait_ge(cx_done, p + 1)
                for c in range(DC):
                    last = nc.tensor.transpose(ps[:, 7, 256 + c * P:256 + c * P + QROWS],
                                               cx[0:QROWS, c * HC:(c + 1) * HC].rearrange("p h d -> p (h d)"),
                                               cst[0:QROWS, C_ID:C_ID + QROWS])
                last.then_inc(ct_mm, 1)

            pe.wait_ge(init_done, 6)
            pe.wait_ge(vt_done, 2)
            pe.wait_ge(q_done, 4)
            scores(0, 0)
            scores(1, 1)
            pe.wait_ge(vt_done, 4)
            pe.wait_ge(k_done, 4)

            def turn(p, par, more):
                pe.wait_ge(s_exp, p + 1)
                after(pe, tr_done, p * 2)
                for g in range(NG):
                    hh = min(G3, H - g * G3)
                    at = PSLOT[g] % G3 * QROWS
                    last = nc.tensor.transpose(
                        ps[0:hh * S, 4 + PSLOT[g] // G3, at:at + QROWS],
                        prob[0:QROWS, par, g * G3:g * G3 + hh].rearrange("p h s -> p (h s)"),
                        cst[0:QROWS, C_ID:C_ID + QROWS])
                last.then_inc(tr_mm, 1)
                pe.wait_ge(v_staged, p * 2 + 2)
                after(pe, v_done, p)
                for u in range(2):
                    for c in range(DC):
                        last = nc.tensor.transpose(
                            ps[0:G3 * S, 6, u * D + c * P:u * D + (c + 1) * P],
                            vst[:, par, c, u], ident)
                last.then_inc(v_mm, 1)
                if not (isinstance(p, int) and p == 0):
                    context_transposed(p - 1)
                if more:
                    scores(p + 2, par)
                pe.wait_ge(v_done, p + 1)
                pe.wait_ge(tr_done, p * 2 + 2)
                after(pe, ct_done, p)
                for u in range(2):
                    for g in range(NG):
                        hh = min(G3, H - g * G3)
                        last = mm(ps[QB * u:QB * u + S, 7, g * G3 * DH:(g * G3 + hh) * DH],
                                  pT[0:hh * S, PSLOT[g], QB * u:QB * u + S],
                                  v3[0:hh * S, u, g * G3 * DH:(g * G3 + hh) * DH])
                last.then_inc(pv_mm, 1)

            over_pairs(pe.Fori, turn)
            context_transposed(PAIRS - 1)

            pe.wait_ge(ct_done, PAIRS)
            for n in range(NH):
                for c in range(DC):
                    for k in range(DC):
                        last = mm(ps[:, 2 * n + c, 0:HT], wo[:, k, c * P:(c + 1) * P],
                                  cT[:, k, n * HT:(n + 1) * HT], k == 0, k == DC - 1)
                    last.then_inc(op_mm, 1)
            mean(ln2, 0, h1, (op_done, 2))
            mean(ln2, 1, h1, (op_done, 4))
            var(ln2, 0)
            var(ln2, 1)
            pe.wait_ge(ld_mlp, 64)
            for n in range(NH):
                pe.wait_ge(ln2.aff, 2 * n + 2)
                for k in range(DC):
                    last = mm(ps[:, n, 0:HT], f1u[:, k], xn[:, k, n * HT:(n + 1) * HT], k == 0, k == DC - 1)
                last.then_inc(z1_mm, 1)
                pe.wait_ge(z1_done, n + 1)
                for f in range(FIC):
                    if n * FIC + f >= 2:
                        pe.wait_ge(hm_done, n * FIC + f - 1)
                    mm(ps[:, 2 + f % 2, 0:HT], f1v[:, f * P:(f + 1) * P], z1[:, n]).then_inc(hm_mm, 1)
                pe.wait_ge(ln2.sd, 2)
                for f in range(FIC):
                    pe.wait_ge(hm_done, n * FIC + f + 1)
                    last = mm(ps[:, 4 + n, 0:HT], f2u[:, f], hm[:, f], f == 0, f == FIC - 1)
                last.then_inc(z2_mm, 1)
                pe.wait_ge(z2_done, n + 1)
                for c in range(DC):
                    if n:
                        pe.wait_ge(mo_done, c + 1)
                    mm(ps[:, 6 + c, 0:HT], f2v[:, c * P:(c + 1) * P], z2[:, n]).then_inc(mo_mm, 1)
            mean(ln3, 0, hs, (mo_done, 2))
            mean(ln3, 1, hs, (mo_done, 4))
            var(ln3, 0)
            var(ln3, 1)
            pe.wait_ge(ln3.aff, 2)
            pe.wait_ge(ld_gate, 16)
            pe.wait_ge(init_done, 6)
            for t in range(TT):
                rows = P if t < TT - 1 else LAST
                for k in range(DC):
                    last = mm(ps[0:rows, 3, 16 * t:16 * t + E], h3[:, k, t * P:t * P + rows], gw[:, k], k == 0, k == DC - 1)
            last.then_inc(lg_mm, 1)

            def down(k, u, par, first=False):
                n, j = u // 2, u % 2
                pe.wait_ge(al_done, k + 1)
                for c in range(DC):
                    last = weight3(lambda w: w[:, par, W1C + j * D + c * P:W1C + j * D + (c + 1) * P],
                                   ps[:, 2 * n + c, 0:HT], w_hi, w_lo, a_hi[:, u], a_lo[:, u],
                                   first, False)
                last.then_inc(y_mm, 1)

            def expert(e, par, turn):
                for u in range(4):
                    k = e * 4 + u
                    n, j = u // 2, u % 2
                    if u == 0:
                        pe.wait_ge(w1_lo_done, e + 1)
                        pe.wait_ge(w2_lo_done, e + 1)
                    if isinstance(e, int) and e == 0 and j == 0:
                        pe.wait_ge(xs_lo, n + 1)
                    if isinstance(k, int) and k == 4 * 0 + 2:
                        pe.wait_ge(gt, 2)
                    if not (isinstance(k, int) and k < 2):
                        pe.wait_ge(t1_done, k - 1)
                    for which, done in ((1, g_mm), (0, x_mm)):
                        for c in range(DC):
                            at = c * 2 * F + which * F + j * P
                            last = weight3(lambda w: w[:, par, at:at + P],
                                           ps[:, 4 + 2 * j + (1 - which), 0:HT], w_hi, w_lo,
                                           x_hi[:, c, n * HT:(n + 1) * HT], x_lo[:, c, n * HT:(n + 1) * HT],
                                           c == 0, c == DC - 1)
                        last.then_inc(done, 1)
                    if u >= 2:
                        down(k - 2, u - 2, par, first=isinstance(e, int) and e == 0 and u == 2)
                    elif not (isinstance(e, int) and e == 0):
                        down(k - 2, u + 2, 1 - par, first=isinstance(e, int) and e == 1 and u == 0)

            over_experts(pe.Fori, expert)
            down(4 * NE - 2, 2, (NE - 1) % 2)
            down(4 * NE - 1, 3, (NE - 1) % 2)
            pe.wait_ge(ld_b2, 16)
            pe.wait_ge(ld_c17, 16)
            for n in range(NH):
                for c in range(DC):
                    mm(ps[:, 2 * n + c, 0:HT], b2_sb[:, c * P:(c + 1) * P],
                       comb17[:, n * HT:(n + 1) * HT], False, True).then_inc(y_fin, 1)
            mean(ln4, 0, hs, (y_done, 2))
            mean(ln4, 1, hs, (y_done, 4))
            var(ln4, 0)
            var(ln4, 1)


def _features(a):
    a = np.asarray(a)
    a = np.moveaxis(a, -1, 0)
    a = a.reshape((a.shape[0] // P, P) + a.shape[1:])
    return np.ascontiguousarray(np.moveaxis(a, 0, 1))


def kernel(**inputs):
    import concourse.bacc as bacc
    from concourse.bass_utils import run_bass_kernel_spmd as run

    a = {k.replace("L0_", ""): np.asarray(v) for k, v in inputs.items()}
    f32 = np.float32
    arrays = {}
    g = IMG // PATCH
    x = a["x"].reshape(B, CH, g, PATCH, g, PATCH).transpose(0, 2, 4, 1, 3, 5).reshape(B * NPATCH, KP * P)
    arrays["patches"] = _features(x)
    arrays["tok_w"] = _features(a["tok_W"])
    cols = [_features(a["tok_b"]), _features(a["tok_pos_embedding"][0]), _features(a["tok_cls_token"][0, 0]),
            _features(a["attn_ln1_g"]), _features(a["attn_ln1_b"]), _features(a["attn_ln2_g"]),
            _features(a["attn_ln2_b"]), _features(a["attn_q_b"].reshape(D)), _features(a["attn_k_b"].reshape(D)),
            _features(a["attn_v_b"].reshape(D)), _features(a["attn_out_b"]), _features(a["attn_fc1_b"]),
            _features(a["attn_fc2_b"])]
    arrays["vecs"] = np.concatenate([c.reshape(P, -1) for c in cols], axis=1)
    p = np.arange(P)[:, None]
    arrays["csts"] = np.concatenate([
        np.eye(P), np.full((P, P), 1.0 / D), (p // DH == np.arange(HC)[None, :]),
        (p // S == (np.arange(D)[None, :] // DH) % G3),
        np.where(np.tile(np.arange(S), HC)[None, :] > p, -1e9, 0.0)], axis=1).astype(f32)
    us, vs = [], []
    for w in "qkv":
        us.append(a[f"attn_{w}_U"].transpose(1, 2, 0).reshape(H // 2, 2 * R, D).transpose(1, 0, 2))
        v = a[f"attn_{w}_V"]
        blk = np.zeros((2 * R, H // 2, 2 * DH), f32)
        for i in range(2):
            blk[i * R:(i + 1) * R, :, i * DH:(i + 1) * DH] = v[i::2].transpose(1, 0, 2)
        vs.append(blk)
    arrays["ut"] = np.stack(us, axis=1)
    arrays["vblk"] = np.stack(vs, axis=1)
    arrays["out_u"] = a["attn_out_U"].T.reshape(2, RO, D).transpose(1, 0, 2)
    arrays["out_v"] = a["attn_out_V"].reshape(2, RO, D).transpose(1, 0, 2)
    arrays["fc1_u"] = a["attn_fc1_U"].reshape(DC, P, R_MLP).transpose(1, 0, 2)
    arrays["fc1_v"] = a["attn_fc1_V"]
    arrays["fc2_u"] = a["attn_fc2_U"].reshape(FIC, P, R_MLP).transpose(1, 0, 2)
    arrays["fc2_v"] = a["attn_fc2_V"]
    arrays["gate"] = _features(a["ffn_gate_w"])
    sw1 = a["ffn_s_fc1_w"].reshape(2, NS, F, D).transpose(1, 0, 2, 3).reshape(NS, 2 * F, D)
    sw2 = a["ffn_s_fc2_w"].reshape(D, NS, F).transpose(1, 0, 2)
    sb1 = a["ffn_s_fc1_b"].reshape(2, NS, F).transpose(1, 0, 2).reshape(NS, 2 * F)
    w1 = np.concatenate([sw1, a["ffn_fc1_w"]])
    w2 = np.concatenate([sw2, a["ffn_fc2_w"]])
    b1 = np.concatenate([sb1, a["ffn_fc1_b"]])
    mult = np.concatenate([a["ffn_s_geglu_mult"].reshape(NS, F), a["ffn_geglu_mult"]])
    packs = []
    for e in range(NE):
        packs.append(np.concatenate([
            w1[e].T.reshape(DC, P, 2 * F).transpose(1, 0, 2).reshape(P, W1C),
            w2[e].T.reshape(F // P, P, D).transpose(1, 0, 2).reshape(P, W2C),
            _features(b1[e][F:]).reshape(P, -1), _features(b1[e][:F]).reshape(P, -1),
            _features(mult[e]).reshape(P, -1)], axis=1))
    arrays["experts"] = np.concatenate(packs)
    arrays["b2"] = np.concatenate([a["ffn_s_fc2_b"][None], np.zeros((NS - 1, D), f32), a["ffn_fc2_b"]])
    arrays = {k: np.ascontiguousarray(v) for k, v in arrays.items()}

    nc = bacc.Bacc("TRN2", target_bir_lowering=False, num_devices=1)
    args = [nc.dram_tensor(k, v.shape, F32, kind="ExternalInput").ap() for k, v in arrays.items()]
    out = nc.dram_tensor("out", (D, T), F32, kind="ExternalOutput").ap()
    comb_dram = nc.dram_tensor("comb_dram", (NE, TPAD), F32, kind="Internal").ap()
    vit_tower_kernel(nc, *args, out, comb_dram)
    r = run(nc, [arrays], core_ids=[0])
    return np.ascontiguousarray(r.results[0]["out"].T.reshape(B, S, D))
```

```python
from contextlib import ExitStack

import numpy as np
import concourse.bass as bass
from concourse import mybir

F32 = mybir.dt.float32
F32R = mybir.dt.float32r
BF16 = mybir.dt.bfloat16
ACT = mybir.ActivationFunctionType
ALU = mybir.AluOpType
AX = mybir.AxisListType

P = 128
B, CH, IMG, PATCH = 16, 3, 96, 16
NPATCH = (IMG // PATCH) ** 2
S = NPATCH + 1
T = B * S
NH = 2
HB = B // NH
HT = T // NH
HP = HB * NPATCH
D = 256
DC = D // P
KP = CH * PATCH * PATCH // P
H, DH, R = 16, 16, 48
HC = P // DH
R_OUT, RO = 192, 96
R_MLP = 128
FI = 4 * D
FIC = FI // P
E, TOPK, F, FS = 15, 3, 256, 512
NS = FS // F
NE = NS + E
W1C, W2C = DC * 2 * F, F // P * D
SMALL = 3 * (F // P)
EXP_COLS = W1C + W2C + SMALL
G3 = 3
NG = (H + G3 - 1) // G3
PAIRS = B // 2
QB = 64
QROWS = QB + S
PSLOT = (0, 1, 2, 4, 5, 3)
TT = 5
LAST = T - (TT - 1) * P
SQ = 32
NQ = P // SQ
QT = HT // NQ
TPAD = TT * P
EPS = 1e-5
OP_BANK = (0, 4)
HM_BANK, Z2_BANK, MO_BANK = 6, 4, 2
WARMS = 9
GATE_STEPS = 9
LOG_COLS = 20

_v = 0


def _col(n):
    global _v
    _v += n
    return _v - n


C_TOKB, C_POS, C_CLS = _col(DC), _col(DC * S), _col(DC)
C_LN1G, C_LN1B, C_LN2G, C_LN2B = _col(DC), _col(DC), _col(DC), _col(DC)
C_QB, C_KB, C_VB, C_OUTB = _col(DC), _col(DC), _col(DC), _col(DC)
C_FC1B, C_FC2B = _col(FIC), _col(DC)
NVEC = _v
_v = 0
C_ID, C_ONES, C_SEL, C_BLK, C_GRP, C_CAUS = _col(P), _col(P), _col(NQ * P), _col(HC), _col(DC * G3), _col(HC * S)
NCST = _v


def vit_tower_kernel(nc, patches, tok_w, vecs, csts, ut, vblk, out_u, out_v, fc1_u, fc1_v, fc2_u, fc2_v,
                     gate, experts, b2, out, comb_dram):
    ctx = ExitStack()
    with ctx:
        def sb(name, shape, dt=F32):
            return ctx.enter_context(nc.sbuf_tensor(name, shape, dt))

        def sem(name):
            return ctx.enter_context(nc.semaphore(name))

        pt_mem = sb("patches_sb", [P, KP * B * NPATCH])
        pt_sb = pt_mem[:, :].rearrange("p (k n) -> p k n", k=KP)
        tw_mem = sb("tok_w_sb", [P, KP * D])
        tw_sb = tw_mem[:, :].rearrange("p (k n) -> p k n", k=KP)
        vec = sb("vec_sb", [P, NVEC])
        cst = sb("cst_sb", [P, NCST])
        ident, ones_d = cst[:, C_ID:C_ID + P], cst[:, C_ONES:C_ONES + P]
        eps_t = sb("eps_t", [P, 1])
        warm_t = sb("warm_t", [P, WARMS])
        ident_bf = sb("ident_bf", [P, S], BF16)
        caus_bf = sb("caus_bf", [P, HC * S], BF16)
        h0 = sb("h0", [P, DC, T])
        xn = sb("xn", [P, DC, T])
        qT = sb("qT", [P, DC, T])
        vT = sb("vT", [P, DC, T])
        kT = sb("kT", [P, DC, T])
        h3 = sb("h3", [P, DC, T])
        ut_mem = sb("ut_sb", [P, 3 * H // 2 * D])
        ut_sb = ut_mem[0:2 * R, :].rearrange("p (i j d) -> p i j d", i=3, j=H // 2)
        vb_sb = sb("vb_sb", [2 * R, 3, H // 2, 2 * DH])
        wqkv = sb("wqkv", [P, 3, DC, D])
        ou_sb = sb("ou_sb", [RO, 2, D])
        ov_sb = sb("ov_sb", [RO, 2, D])
        wo = sb("wo", [P, DC, D])
        xc = sb("ln_xc", [P, NH, DC, HT])
        sq = sb("ln_sq", [P, NH, DC, HT])
        sd = sb("ln_sd", [P, NH, QT])
        rs = sb("ln_rs", [P, NH, QT])
        fill = sb("fill", [P, HT], BF16)
        qst = sb("qst", [P, 2, DC, 2 * S])
        vst = sb("vst", [P, 2, DC, 2, G3 * S])
        soft_mem = sb("soft_mem", [P, 4 * H * S])
        dsc, prob = (soft_mem[:, i * 2 * H * S:(i + 1) * 2 * H * S].rearrange("p (a h s) -> p a h s", a=2, h=H)
                     for i in range(2))
        wT = soft_mem[:, 0:3 * DC * D].rearrange("p (i c d) -> p i c d", i=3, c=DC)
        mx = sb("mx", [P, 2, H])
        sm = sb("sm", [P, 2, H])
        rsm = sb("rsm", [P, 2, H])
        pT = sb("pT", [G3 * S, NG, QROWS])
        v3 = sb("v3", [G3 * S, 2, D])
        cx = sb("cx", [P, H, DH])
        f1u = sb("f1u", [P, DC, R_MLP])
        f1v = sb("f1v", [P, FI])
        f2u = sb("f2u", [P, FIC, R_MLP])
        f2v = sb("f2v", [P, D])
        gw = sb("gw", [P, DC, E])
        lg = sb("lg", [P, TT, LOG_COLS])
        top = sb("top", [P, TT, 8])
        rep = sb("rep", [P, TT, LOG_COLS])
        g1 = sb("g1", [P, TT])
        g2 = sb("g2", [P, TT])
        comb = sb("comb", [P, TT, 32])
        combT = sb("combT", [P, TT, 32])
        comb17 = sb("comb17", [NE, T])
        b2_sb = sb("b2_sb", [NE, D])
        x_hi = sb("x_hi", [P, DC, T], F32R)
        x_lo = sb("x_lo", [P, DC, T], F32R)
        stage = sb("stage", [P, 2, EXP_COLS])
        small = sb("small", [P, 2, SMALL])
        w_hi = sb("w_hi", [P, 2, W1C + W2C], F32R)
        w_lo = sb("w_lo", [P, 2, W1C + W2C], F32R)
        cb = sb("cb", [P, 2, T])
        ones_t = sb("ones_t", [P, HT])
        t1 = sb("t1", [P, 2, HT])
        t2 = sb("t2", [P, 2, HT])
        a_hi = sb("a_hi", [P, 4, HT], F32R)
        a_lo = sb("a_lo", [P, 4, HT], F32R)

        at = 2 * 2 * DC * HC * S
        kblk = ut_mem[:, 0:at].rearrange("p (a u c h s) -> p a u c h s", a=2, u=2, c=DC, h=HC)
        cT, h1, hs = (ut_mem[:, at + i * DC * T:at + (i + 1) * DC * T].rearrange("p (c t) -> p c t", c=DC)
                      for i in range(3))
        hm = pt_mem[:, 0:FIC * HT].rearrange("p (f t) -> p f t", f=FIC)
        gel = pt_mem[:, FIC * HT:(FIC + 2) * HT].rearrange("p (j t) -> p j t", j=2)
        z1 = tw_mem[:, 0:T].rearrange("p (n t) -> p n t", n=NH)
        z2 = tw_mem[:, T:2 * T].rearrange("p (n t) -> p n t", n=NH)

        ps = ctx.enter_context(nc.psum_tensor("ps", [P, 8, 512], F32))

        ld_patch = [sem(f"ld_patch{k}") for k in range(KP)]
        ld_cst, ld_vec, ld_out = sem("ld_cst"), sem("ld_vec"), sem("ld_out_w")
        ld_qkv = [sem(f"ld_qkv{i}") for i in range(3)]
        ld_mlp, ld_gate, ld_b2 = sem("ld_mlp"), sem("ld_gate"), sem("ld_b2")
        ld_exp = [sem("ld_exp0"), sem("ld_exp1")]
        ld_cb = [sem("ld_cb0"), sem("ld_cb1")]
        ld_c17 = sem("ld_c17")
        st_comb, st_out = sem("st_comb"), sem("st_out")
        fill_done = sem("fill_done")
        init_done, warmed = sem("init_done"), sem("warmed")
        emb_mm, emb_done = sem("emb_mm"), sem("emb_done")
        cmp_mm, wt_out, wt_mm, cmp_done = sem("cmp_mm"), sem("wt_out"), sem("wt_mm"), sem("cmp_done")
        pr_mm, q_done, k_done, vt_done = sem("proj_mm"), sem("q_done"), sem("k_done"), sem("vt_done")
        staged, k11_staged, q_staged, v_staged = sem("staged"), sem("k11_staged"), sem("q_staged"), sem("v_staged")
        s_mm, s_max, s_cen, s_exp, s_sum, s_rec = (sem(n) for n in ("s_mm", "s_max", "s_cen", "s_exp", "s_sum", "s_rec"))
        v_mm, v_done, tr_mm, tr_done = sem("v_mm"), sem("v_done"), sem("tr_mm"), sem("tr_done")
        pv_mm, cx_done, ct_mm, ct_done = sem("pv_mm"), sem("cx_done"), sem("ct_mm"), sem("ct_done")
        op_mm, op_done = sem("op_mm"), sem("op_done")
        sum_done = sem("sum_done")
        z1_mm, z1_done, hm_mm, hm_done = sem("z1_mm"), sem("z1_done"), sem("hm_mm"), sem("hm_done")
        z2_mm, z2_done, mo_mm, mo_done = sem("z2_mm"), sem("z2_done"), sem("mo_mm"), sem("mo_done")
        lg_mm, gt, top_done = sem("lg_mm"), sem("gate_chain"), sem("top_done")
        gt_exp = sem("gate_exp")
        xs_hi, xs_lo = sem("xs_hi"), sem("xs_lo")
        w1_hi_done, w2_hi_done, w1_lo_done, w2_lo_done = sem("w1_hi"), sem("w2_hi"), sem("w1_lo"), sem("w2_lo")
        small_done = sem("small_done")
        g_mm, x_mm, gel_done, t1_done, t2_done = sem("g_mm"), sem("x_mm"), sem("gel_done"), sem("t1_done"), sem("t2_done")
        ah_done, al_done, y_mm = sem("ah_done"), sem("al_done"), sem("y_mm")
        y_done = sem("y_done")

        class Norm:

            def __init__(self, name, *banks):
                self.banks = banks
                self.mean, self.cen, self.sq = sem(name + "_mean"), sem(name + "_cen"), sem(name + "_sq")
                self.var, self.sd, self.rs = sem(name + "_var"), sem(name + "_sd"), sem(name + "_rs")
                self.bc, self.out, self.aff = sem(name + "_bc"), sem(name + "_out"), sem(name + "_aff")

        ln1, ln2, ln3, ln4 = Norm("ln1", 6, 7), Norm("ln2", 2, 3), Norm("ln3", 0, 1), Norm("ln4", 4, 5)
        VAR = 384

        def half(t, n):
            return t[:, :, n * HT:(n + 1) * HT]

        def mm(o, w, x, start=True, stop=True):
            return nc.tensor.matmul(o, w, x, start=start, stop=stop)

        def weight3(w, o, w_h, w_l, x_h, x_l, first, last):
            mm(o, w(w_h), x_h, start=first, stop=False)
            mm(o, w(w_h), x_l, start=False, stop=False)
            return mm(o, w(w_l), x_h, start=False, stop=last)

        def over_pairs(fori, turn):
            turn(0, 0, 3)
            with fori(0, 2) as i:
                turn(i * 2 + 1, 1, 3)
                turn(i * 2 + 2, 0, 3)
            turn(5, 1, 2)
            turn(6, 0, 1)
            turn(7, 1, 0)

        def keys_block(eng, p, par, u, c):
            return eng.tensor_tensor(
                kblk[:, par, u, c],
                kT[:, c, bass.ds(p * (2 * S) + u * S, S)].unsqueeze(1).to_broadcast([P, HC, S]),
                cst[:, C_BLK:C_BLK + HC].unsqueeze(2).to_broadcast([P, HC, S]), ALU.mult)

        def after(eng, semaphore, count):
            if not (isinstance(count, int) and count == 0):
                eng.wait_ge(semaphore, count)

        def over_experts(fori, expert):
            expert(0, 0, 0)
            expert(1, 1, 0)
            with fori(0, (NE - 3) // 2) as i:
                expert(i * 2 + 2, 0, i + 1)
                expert(i * 2 + 3, 1, i + 1)
            expert(NE - 1, 0, (NE - 1) // 2)

        def over_units(fori, unit):
            for k in range(8):
                unit(k, k % 4, k // 2 % 2, k // 2 % 2, 0, k // 4, k in (0, 2))

            def expert(e, par, turn):
                for u in range(4):
                    unit(e * 4 + u, u, e, par, turn, u // 2, u == 0)

            with fori(0, (NE - 3) // 2) as i:
                expert(i * 2 + 2, 0, i + 1)
                expert(i * 2 + 3, 1, i + 1)
            expert(NE - 1, 0, (NE - 1) // 2)

        def is_unit(k, count):
            return isinstance(k, int) and k == count

        PROJ_BANK = (4, 5, 6, 7, 0, 1, 4, 5, 6, 7, 4, 5)

        block = ctx.enter_context(nc.Block())

        @block.sync
        def _(sp):
            for k in range(KP):
                sp.dma_start(tw_sb[:, k], tok_w[:, k]).then_inc(ld_patch[k], 16)
                sp.dma_start(pt_sb[:, k], patches[:, k]).then_inc(ld_patch[k], 16)
            sp.dma_start(vec[:, :], vecs).then_inc(ld_vec, 16)
            sp.dma_start(cst[:, :], csts).then_inc(ld_cst, 16)
            for i in range(3):
                sp.dma_start(ut_sb[:, i], ut[:, i]).then_inc(ld_qkv[i], 16)
                sp.dma_start(vb_sb[:, i], vblk[:, i]).then_inc(ld_qkv[i], 16)
            sp.dma_start(ou_sb[:, :], out_u).then_inc(ld_out, 16)
            sp.dma_start(ov_sb[:, :], out_v).then_inc(ld_out, 16)
            sp.dma_start(f1u[:, :], fc1_u).then_inc(ld_mlp, 16)
            sp.dma_start(f1v[:, :], fc1_v).then_inc(ld_mlp, 16)
            sp.dma_start(f2u[:, :], fc2_u).then_inc(ld_mlp, 16)
            sp.dma_start(f2v[:, :], fc2_v).then_inc(ld_mlp, 16)
            sp.dma_start(gw[:, :], gate).then_inc(ld_gate, 16)
            sp.dma_start(b2_sb[:, :], b2).then_inc(ld_b2, 16)

            def load_expert(e, par):
                if not (isinstance(e, int) and e < 2):
                    sp.wait_ge(small_done, e - 1)
                sp.dma_start(stage[:, par], experts[bass.ds(e * P, P), :]).then_inc(ld_exp[par], 16)

            for e in range(4):
                load_expert(e, e % 2)
            sp.wait_ge(gt, GATE_STEPS)
            for q in range(4):
                rows = comb_dram.rearrange("e (t q c) -> e t q c", q=4, c=32)[:, :, q, :]
                sp.dma_start(rows, combT[32 * q:32 * q + NE, :, :]).then_inc(st_comb, 16)
            sp.wait_ge(st_comb, 64)

            def load_weights(e, par):
                sp.wait_ge(t2_done, 4 * (e - 1))
                sp.dma_start(cb[:, par], comb_dram[bass.ds(e, 1), 0:T].to_broadcast([P, T])) \
                    .then_inc(ld_cb[par], 16)

            with sp.Fori(0, (NE - 5) // 2) as i:
                for par in range(2):
                    load_weights(i * 2 + 2 + par, par)
                    load_expert(i * 2 + 4 + par, par)
            load_weights(NE - 3, 0)
            load_expert(NE - 1, 0)
            sp.dma_start(comb17[:, :], comb_dram[:, 0:T]).then_inc(ld_c17, 16)
            load_weights(NE - 2, 1)
            load_weights(NE - 1, 0)

            for n in range(NH):
                for c in range(DC):
                    sp.wait_ge(ln4.out, DC * n + c + 1)
                    sp.dma_start(out[c * P:(c + 1) * P, n * HT:(n + 1) * HT], sq[:, n, c]).then_inc(st_out, 16)
            sp.wait_ge(st_out, 16 * NH * DC)

        @block.gpsimd
        def _(pool):
            def stage_keys(p, par):
                if not (isinstance(p, int) and p < 2):
                    pool.wait_ge(s_mm, p - 1)
                for u, c in ((0, 0), (0, 1), (1, 0)):
                    keys_block(nc.gpsimd, p, par, u, c).then_inc(staged, 1)

            def stage_values(p, par):
                if isinstance(p, int):
                    pool.wait_ge(vt_done, 2 if p < PAIRS // 2 else 4)
                if not (isinstance(p, int) and p < 2):
                    pool.wait_ge(v_mm, p - 1)
                for c in range(DC):
                    for u in range(2):
                        pool.tensor_tensor(
                            vst[:, par, c, u].rearrange("p (r s) -> p r s", r=G3),
                            vT[:, c, bass.ds(p * (2 * S) + u * S, S)].unsqueeze(1).to_broadcast([P, G3, S]),
                            cst[:, C_GRP + c * G3:C_GRP + (c + 1) * G3].unsqueeze(2).to_broadcast([P, G3, S]),
                            ALU.mult).then_inc(v_staged, 1)

            pool.wait_ge(ld_cst, 16)
            pool.wait_ge(k_done, 2)
            stage_keys(0, 0)
            stage_keys(1, 1)
            stage_values(0, 0)
            stage_values(1, 1)
            stage_keys(2, 0)

            def turn(p, par, ahead):
                if ahead >= 3:
                    stage_keys(p + 3, 1 - par)
                if ahead >= 2:
                    stage_values(p + 2, par)
                if isinstance(p, int) and p == 0:
                    pool.wait_ge(k_done, 4)
                    pool.wait_ge(vt_done, 4)

            over_pairs(pool.Fori, turn)

            for n in range(NH):
                pool.wait_ge(op_done, DC * (n + 1))
                pool.tensor_tensor(half(hs, n), half(h0, n), half(h1, n), ALU.add).then_inc(sum_done, 1)

            def split_lo(e, par, turn):
                pool.wait_ge(w1_hi_done, e + 1)
                if not (isinstance(e, int) and e < 2):
                    pool.wait_ge(x_mm, 4 * (e - 1))
                pool.tensor_tensor(w_lo[:, par, 0:W1C], stage[:, par, 0:W1C],
                                   w_hi[:, par, 0:W1C].bitcast(F32), ALU.subtract).then_inc(w1_lo_done, 1)
                pool.wait_ge(w2_hi_done, e + 1)
                if not (isinstance(e, int) and e < 2):
                    pool.wait_ge(y_mm, 4 * (e - 1))
                pool.tensor_tensor(w_lo[:, par, W1C:W1C + W2C], stage[:, par, W1C:W1C + W2C],
                                   w_hi[:, par, W1C:W1C + W2C].bitcast(F32), ALU.subtract).then_inc(w2_lo_done, 1)
                pool.tensor_copy(small[:, par], stage[:, par, W1C + W2C:EXP_COLS]).then_inc(small_done, 1)

            over_experts(pool.Fori, split_lo)

        @block.scalar
        def _(act):
            def squares(ln, n):
                act.wait_ge(ln.cen, n + 1)
                nc.scalar.activation(sq[:, n], xc[:, n], ACT.Square).then_inc(ln.sq, 1)

            def std(ln, n):
                act.wait_ge(ln.var, n + 1)
                nc.scalar.activation(sd[:, n], ps[:, ln.banks[n], VAR:VAR + QT], ACT.Sqrt,
                                     bias=eps_t[:, 0:1]).then_inc(ln.sd, 1)

            def warm(function):
                i = next(warms)
                nc.scalar.activation(warm_t[:, i:i + 1], eps_t[:, 0:1], function).then_inc(warmed, 1)

            warms = iter(range(WARMS))

            def affine_act(ln, n, gamma, beta):
                for c in range(DC):
                    act.wait_ge(ln.out, DC * n + c + 1)
                    nc.scalar.activation(xn[:, c, n * HT:(n + 1) * HT], sq[:, n, c], ACT.Identity,
                                         bias=vec[:, beta + c:beta + c + 1],
                                         scale=vec[:, gamma + c:gamma + c + 1]).then_inc(ln.aff, 1)

            def w1_hi(e, par, turn):
                act.wait_ge(ld_exp[par], 16 * (turn + 1))
                if not (isinstance(e, int) and e < 2):
                    act.wait_ge(x_mm, 6 if isinstance(e, int) and e == 2 else 4 * (e - 1))
                nc.scalar.activation(w_hi[:, par, 0:W1C], stage[:, par, 0:W1C], ACT.Copy).then_inc(w1_hi_done, 1)

            def w2_hi(e, par, turn):
                if not (isinstance(e, int) and e < 2):
                    act.wait_ge(y_mm, 6 if isinstance(e, int) and e == 2 else 4 * (e - 1))
                nc.scalar.activation(w_hi[:, par, W1C:W1C + W2C], stage[:, par, W1C:W1C + W2C],
                                     ACT.Copy).then_inc(w2_hi_done, 1)

            act.wait_ge(ld_vec, 16)
            act.wait_ge(init_done, 2)
            warm(ACT.Sqrt)
            squares(ln1, 0)
            squares(ln1, 1)
            std(ln1, 0)
            std(ln1, 1)
            for i in range(3):
                act.wait_ge(wt_mm, i + 1)
                nc.scalar.activation(wqkv[:, i].rearrange("p c d -> p (c d)"), ps[:, i, :], ACT.Copy) \
                    .then_inc(cmp_done, 1)
            affine_act(ln1, 0, C_LN1G, C_LN1B)
            affine_act(ln1, 1, C_LN1G, C_LN1B)
            def projection_out(n, dst, bias, done, first):
                for c in range(DC):
                    act.wait_ge(pr_mm, first + c + 1)
                    nc.scalar.activation(dst[:, c, n * HT:(n + 1) * HT], ps[:, PROJ_BANK[first + c], 0:HT],
                                         ACT.Identity, bias=vec[:, bias + c:bias + c + 1]).then_inc(done, 1)

            def stage_queries(p, par):
                if not (isinstance(p, int) and p < 2):
                    act.wait_ge(s_mm, p - 1)
                nc.scalar.activation(qst[:, par], qT[:, :, bass.ds(p * (2 * S), 2 * S)], ACT.Copy) \
                    .then_inc(q_staged, 1)

            def exps(p, par):
                act.wait_ge(s_cen, p + 1)
                if not (isinstance(p, int) and p < 2):
                    act.wait_ge(tr_mm, p - 1)
                    act.wait_ge(s_sum, p - 1)
                nc.scalar.activation(prob[0:QROWS, par], dsc[0:QROWS, par], ACT.Exp,
                                     scale=DH ** -0.5).then_inc(s_exp, 1)

            def context_out(p):
                act.wait_ge(ct_mm, p + 1)
                nc.scalar.activation(
                    cT[:, :, bass.ds(p * (2 * S), 2 * S)].rearrange("p c (u s) -> p c u s", u=2),
                    ps[:, 7, 256:256 + DC * P].rearrange("p (c u s) -> p c u s", c=DC, u=2)[:, :, :, 0:S],
                    ACT.Copy).then_inc(ct_done, 1)

            projection_out(0, qT, C_QB, q_done, 0)
            act.wait_ge(q_done, 2)
            stage_queries(0, 0)
            stage_queries(1, 1)
            projection_out(0, vT, C_VB, vt_done, 4)
            act.wait_ge(cmp_mm, 4)
            nc.scalar.activation(wo[:, :].rearrange("p c d -> p (c d)"), ps[:, 3, :], ACT.Copy).then_inc(cmp_done, 1)
            projection_out(1, qT, C_QB, q_done, 6)
            warm(ACT.Exp)
            exps(0, 0)
            stage_queries(2, 0)
            projection_out(1, vT, C_VB, vt_done, 10)
            act.wait_ge(q_done, 4)

            def turn(p, par, ahead):
                act.wait_ge(tr_mm, p + 1)
                after(act, pv_mm, p)
                for k in range(2):
                    nc.scalar.activation(pT[:, k * G3:(k + 1) * G3].rearrange("p g q -> p (g q)"),
                                         ps[0:G3 * S, 4 + k, 0:G3 * QROWS], ACT.Copy).then_inc(tr_done, 1)
                if not (isinstance(p, int) and p == 0):
                    context_out(p - 1)
                act.wait_ge(v_mm, p + 1)
                after(act, pv_mm, p)
                nc.scalar.activation(v3[:, :].rearrange("p u d -> p (u d)"), ps[0:G3 * S, 6, :], ACT.Copy) \
                    .then_inc(v_done, 1)
                if ahead >= 1:
                    exps(p + 1, 1 - par)
                if ahead == 1:
                    warm(ACT.Sqrt)
                if ahead >= 3:
                    stage_queries(p + 3, 1 - par)

            over_pairs(act.Fori, turn)
            squares(ln2, 0)
            context_out(PAIRS - 1)
            std(ln2, 0)
            affine_act(ln2, 0, C_LN2G, C_LN2B)
            w1_hi(0, 0, 0)
            w2_hi(0, 0, 0)
            warm(ACT.Gelu_apprx_tanh)

            def mlp_gelu(g):
                f = g % FIC
                act.wait_ge(hm_mm, g + 1)
                nc.scalar.activation(hm[:, f], ps[:, HM_BANK + g % 2, 0:HT], ACT.Gelu_apprx_tanh,
                                     bias=vec[:, C_FC1B + f:C_FC1B + f + 1]).then_inc(hm_done, 1)

            for g in range(NH * FIC):
                mlp_gelu(g)
                if g == 0:
                    squares(ln2, 1)
                if g == 1:
                    warm(ACT.Sqrt)
                    std(ln2, 1)
                if g == 3:
                    affine_act(ln2, 1, C_LN2G, C_LN2B)
                if g == 6:
                    w1_hi(1, 1, 0)
                if g == 9:
                    w2_hi(1, 1, 0)
                if g == 12:
                    squares(ln3, 0)
            warm(ACT.Sqrt)
            std(ln3, 0)

            def input_hi(n):
                for c in range(DC):
                    act.wait_ge(ln3.aff, DC * n + c + 1)
                    nc.scalar.activation(x_hi[:, c, n * HT:(n + 1) * HT], h3[:, c, n * HT:(n + 1) * HT],
                                         ACT.Copy).then_inc(xs_hi, 1)

            input_hi(0)
            squares(ln3, 1)
            std(ln3, 1)
            warm(ACT.Gelu)

            def act_hi(k, u):
                act.wait_ge(t2_done, k + 1)
                if not (isinstance(k, int) and k < 4):
                    act.wait_ge(y_mm, k - 3)
                nc.scalar.activation(a_hi[:, u], t2[:, u % 2], ACT.Copy).then_inc(ah_done, 1)

            def unit(k, u, e, par, turn, n, first):
                j = u % 2
                act.wait_ge(g_mm, k + 1)
                if not (isinstance(k, int) and k < 2):
                    act.wait_ge(t1_done, k - 1)
                if first:
                    act.wait_ge(small_done, e + 1)
                nc.scalar.activation(gel[:, j], ps[:, 4 + 2 * j, 0:HT], ACT.Gelu,
                                     bias=small[:, par, j:j + 1]).then_inc(gel_done, 1)
                if not is_unit(k, 0):
                    act_hi(k - 1, (u - 1) % 4)
                if is_unit(k, 1):
                    input_hi(1)
                if is_unit(k, 2):
                    act.wait_ge(gt, 2)
                    nc.scalar.activation(lg[:, :, 0:E], lg[:, :, 0:E], ACT.Exp).then_inc(gt_exp, 1)
                    warm(ACT.Gelu)
                if is_unit(k, 5):
                    w1_hi(2, 0, 1)
                if is_unit(k, 7):
                    w2_hi(2, 0, 1)
                if not (isinstance(k, int)):
                    if u == 0:
                        w1_hi(e + 1, 1 - par, turn + par)
                    if u == 2:
                        w2_hi(e + 1, 1 - par, turn + par)

            over_units(act.Fori, unit)
            act_hi(4 * NE - 1, 3)
            warm(ACT.Sqrt)
            squares(ln4, 0)
            squares(ln4, 1)
            std(ln4, 0)
            std(ln4, 1)

        @block.vector
        def _(dve):
            nc.vector.memset(fill[:, :], 0.0).then_inc(fill_done, 1)
            nc.vector.memset(eps_t[:, :], EPS).then_inc(init_done, 1)
            nc.vector.memset(ones_t[:, :], 1.0).then_inc(init_done, 1)
            nc.vector.memset(comb[:, :, :], 1.0).then_inc(init_done, 1)
            nc.vector.memset(lg[:, :, :], -1.0).then_inc(init_done, 1)
            dve.wait_ge(ld_cst, 16)
            nc.vector.tensor_copy(ident_bf[:, :], cst[:, C_ID:C_ID + S]).then_inc(init_done, 1)
            nc.vector.tensor_copy(caus_bf[:, :], cst[:, C_CAUS:C_CAUS + HC * S]).then_inc(init_done, 1)
            dve.wait_ge(ld_vec, 16)
            pos = vec[:, C_POS:C_POS + DC * S].rearrange("p (c s) -> p c s", c=DC)
            for c in range(DC):
                hv = h0[:, c, :].rearrange("p (b s) -> p b s", b=B)
                nc.vector.tensor_scalar(hv[:, :, 0], pos[:, c, 0:1].to_broadcast([P, B]),
                                        vec[:, C_CLS + c:C_CLS + c + 1], None, ALU.add).then_inc(emb_done, 1)
            for n in range(NH):
                for c in range(DC):
                    dve.wait_ge(emb_mm, 2 * n + c + 1)
                    hv = h0[:, c, :].rearrange("p (b s) -> p b s", b=B)
                    nc.vector.scalar_tensor_tensor(
                        hv[:, n * HB:(n + 1) * HB, 1:S],
                        ps[:, 2 * n + c, 0:HP].rearrange("p (b s) -> p b s", b=HB),
                        vec[:, C_TOKB + c:C_TOKB + c + 1],
                        pos[:, c, 1:S].unsqueeze(1).to_broadcast([P, HB, NPATCH]),
                        ALU.add, ALU.add).then_inc(emb_done, 1)

            def centre(ln, n, src):
                dve.wait_ge(ln.mean, n + 1)
                nc.vector.tensor_tensor(
                    xc[:, n], half(src, n),
                    ps[:, ln.banks[n], 0:HT].unsqueeze(1).to_broadcast([P, DC, HT]),
                    ALU.subtract).then_inc(ln.cen, 1)

            def inverse_std(ln, n):
                dve.wait_ge(ln.sd, n + 1)
                nc.vector.reciprocal(rs[:, n], sd[:, n]).then_inc(ln.rs, 1)

            def scale(ln, n):
                dve.wait_ge(ln.bc, n + 1)
                for c in range(DC):
                    nc.vector.tensor_tensor(sq[:, n, c], xc[:, n, c], ps[:, ln.banks[n], 0:HT],
                                            ALU.mult).then_inc(ln.out, 1)

            centre(ln1, 0, h0)
            centre(ln1, 1, h0)
            for i in range(3):
                dve.wait_ge(cmp_mm, i + 1)
                nc.vector.tensor_copy(wT[:, i].rearrange("p c d -> p (c d)"), ps[:, i, :]).then_inc(wt_out, 1)
            inverse_std(ln1, 0)
            inverse_std(ln1, 1)
            scale(ln1, 0)
            scale(ln1, 1)
            def keys_out(n):
                for c in range(DC):
                    g = 6 * n + 2 + c
                    dve.wait_ge(pr_mm, g + 1)
                    nc.vector.tensor_scalar(kT[:, c, n * HT:(n + 1) * HT], ps[:, PROJ_BANK[g], 0:HT],
                                            vec[:, C_KB + c:C_KB + c + 1], None, ALU.add).then_inc(k_done, 1)

            def by_head(par):
                return ps[0:QROWS, 2 * par:2 * par + 2, 0:HC * S].rearrange("p c (h s) -> p c h s", h=HC)

            def maxima(p, par):
                dve.wait_ge(s_mm, p + 1)
                nc.vector.tensor_reduce(mx[0:QROWS, par].rearrange("p (c h) -> p c h", c=DC), by_head(par),
                                        AX.X, ALU.max).then_inc(s_max, 1)

            def centred(p, par):
                if not (isinstance(p, int) and p < 2):
                    dve.wait_ge(s_exp, p - 1)
                dve.wait_ge(s_max, p + 1)
                nc.vector.tensor_tensor(
                    dsc[0:QROWS, par].rearrange("p (c h) s -> p c h s", c=DC), by_head(par),
                    mx[0:QROWS, par].rearrange("p (c h) -> p c h", c=DC).unsqueeze(3)
                    .to_broadcast([QROWS, DC, HC, S]), ALU.subtract).then_inc(s_cen, 1)

            def sums(p, par):
                dve.wait_ge(s_exp, p + 1)
                nc.vector.tensor_reduce(sm[0:QROWS, par], prob[0:QROWS, par], AX.X, ALU.add).then_inc(s_sum, 1)
                dve.wait_ge(s_sum, p + 1)
                nc.vector.reciprocal(rsm[0:QROWS, par], sm[0:QROWS, par]).then_inc(s_rec, 1)

            def key_block(p, par):
                if not (isinstance(p, int) and p < 2):
                    dve.wait_ge(s_mm, p - 1)
                keys_block(nc.vector, p, par, 1, 1).then_inc(k11_staged, 1)

            keys_out(0)
            dve.wait_ge(k_done, 2)
            key_block(0, 0)
            key_block(1, 1)
            maxima(0, 0)
            centred(0, 0)
            keys_out(1)
            maxima(1, 1)
            centred(1, 1)
            key_block(2, 0)
            sums(0, 0)

            def attention_out(n):
                for c in range(DC):
                    dve.wait_ge(op_mm, 2 * n + c + 1)
                    nc.vector.scalar_tensor_tensor(
                        h1[:, c, n * HT:(n + 1) * HT], ps[:, OP_BANK[n] + c, 0:HT],
                        vec[:, C_OUTB + c:C_OUTB + c + 1],
                        h0[:, c, n * HT:(n + 1) * HT], ALU.add, ALU.add).then_inc(op_done, 1)

            def turn(p, par, ahead):
                if ahead >= 3:
                    key_block(p + 3, 1 - par)
                if ahead >= 2:
                    maxima(p + 2, par)
                if ahead == 0:
                    centre(ln2, 0, h1)
                dve.wait_ge(s_rec, p + 1)
                dve.wait_ge(pv_mm, p + 1)
                after(dve, ct_mm, p)
                nc.vector.tensor_tensor(
                    cx[0:QROWS], ps[0:QROWS, 7, 0:D].rearrange("p (h d) -> p h d", h=H),
                    rsm[0:QROWS, par].unsqueeze(2).to_broadcast([QROWS, H, DH]), ALU.mult).then_inc(cx_done, 1)
                if ahead >= 2:
                    centred(p + 2, par)
                if ahead >= 1:
                    sums(p + 1, 1 - par)
                if ahead == 1:
                    attention_out(0)

            over_pairs(dve.Fori, turn)
            inverse_std(ln2, 0)
            scale(ln2, 0)
            attention_out(1)

            def mlp_out(n):
                for c in range(DC):
                    dve.wait_ge(mo_mm, 2 * n + c + 1)
                    nc.vector.scalar_tensor_tensor(
                        hs[:, c, n * HT:(n + 1) * HT], ps[:, MO_BANK + c, 0:HT], vec[:, C_FC2B + c:C_FC2B + c + 1],
                        hs[:, c, n * HT:(n + 1) * HT], ALU.add, ALU.add).then_inc(mo_done, 1)

            def z1_out(n):
                dve.wait_ge(z1_mm, n + 1)
                nc.vector.tensor_copy(z1[:, n], ps[:, n, 0:HT]).then_inc(z1_done, 1)

            def z2_out(n):
                dve.wait_ge(z2_mm, n + 1)
                nc.vector.tensor_copy(z2[:, n], ps[:, Z2_BANK + n, 0:HT]).then_inc(z2_done, 1)

            z1_out(0)
            centre(ln2, 1, h1)
            inverse_std(ln2, 1)
            scale(ln2, 1)
            z1_out(1)
            z2_out(0)
            dve.wait_ge(sum_done, NH)
            mlp_out(0)
            centre(ln3, 0, hs)
            z2_out(1)
            inverse_std(ln3, 0)
            mlp_out(1)

            def scale_h3(n):
                dve.wait_ge(ln3.bc, n + 1)
                for c in range(DC):
                    nc.vector.tensor_tensor(h3[:, c, n * HT:(n + 1) * HT], xc[:, n, c], ps[:, ln3.banks[n], 0:HT],
                                            ALU.mult).then_inc(ln3.aff, 1)

            def input_lo(n):
                for c in range(DC):
                    dve.wait_ge(xs_hi, DC * n + c + 1)
                    nc.vector.tensor_tensor(x_lo[:, c, n * HT:(n + 1) * HT], h3[:, c, n * HT:(n + 1) * HT],
                                            x_hi[:, c, n * HT:(n + 1) * HT].bitcast(F32),
                                            ALU.subtract).then_inc(xs_lo, 1)

            scale_h3(0)
            centre(ln3, 1, hs)
            input_lo(0)
            inverse_std(ln3, 1)
            scale_h3(1)

            def link(ins):
                ins.then_inc(gt, 1)

            def softmax_start():
                dve.wait_ge(lg_mm, 1)
                lps = ps[:, 3, 0:TT * 16].rearrange("p (t e) -> p t e", t=TT)[:, :, 0:E]
                link(nc.vector.tensor_reduce(g1[:, :], lps, AX.X, ALU.max))
                dve.wait_ge(gt, 1)
                link(nc.vector.tensor_tensor(lg[:, :, 0:E], lps, g1[:, :].unsqueeze(2).to_broadcast([P, TT, E]),
                                             ALU.subtract))

            def softmax_end():
                dve.wait_ge(gt_exp, 1)
                link(nc.vector.tensor_reduce(g1[:, :], lg[:, :, 0:E], AX.X, ALU.add))
                dve.wait_ge(gt, 3)
                link(nc.vector.reciprocal(g2[:, :], g1[:, :]))
                dve.wait_ge(gt, 4)
                link(nc.vector.tensor_tensor(lg[:, :, 0:E], lg[:, :, 0:E],
                                             g2[:, :].unsqueeze(2).to_broadcast([P, TT, E]), ALU.mult))
                dve.wait_ge(gt, 5)
                for t in range(TT):
                    nc.vector.max(top[:, t], lg[:, t]).then_inc(top_done, 1)

            def select():
                dve.wait_ge(top_done, TT)
                nc.vector.memset(top[:, :, TOPK:8], -1.0).then_inc(top_done, 1)
                link(nc.vector.tensor_reduce(g1[:, :], top[:, :, 0:TOPK], AX.X, ALU.add))
                dve.wait_ge(top_done, TT + 1)
                for t in range(TT):
                    nc.vector.match_replace(rep[:, t], top[:, t], lg[:, t], 0.0).then_inc(top_done, 1)

            def renorm():
                dve.wait_ge(gt, 6)
                nc.vector.tensor_scalar(g2[:, :], g1[:, :], 1e-20, None, ALU.add).then_inc(top_done, 1)
                dve.wait_ge(top_done, 2 * TT + 2)
                link(nc.vector.reciprocal(g1[:, :], g2[:, :]))
                nc.vector.tensor_tensor(rep[:, :, 0:E], lg[:, :, 0:E], rep[:, :, 0:E], ALU.subtract) \
                    .then_inc(top_done, 1)
                dve.wait_ge(gt, 7)
                dve.wait_ge(top_done, 2 * TT + 3)
                link(nc.vector.tensor_tensor(comb[:, :, NS:NE], rep[:, :, 0:E],
                                             g1[:, :].unsqueeze(2).to_broadcast([P, TT, E]), ALU.mult))
                dve.wait_ge(gt, 8)
                link(nc.vector.transpose(combT[:, :, :].rearrange("p t c -> p (t c)"),
                                         comb[:, :, :].rearrange("p t c -> p (t c)")))

            routing = {1: softmax_start, 2: softmax_end, 3: select, 4: renorm}

            def act_lo(k, u):
                dve.wait_ge(ah_done, k + 1)
                nc.vector.tensor_tensor(a_lo[:, u], t2[:, u % 2], a_hi[:, u].bitcast(F32),
                                        ALU.subtract).then_inc(al_done, 1)

            def unit(k, u, e, par, turn, n, first):
                j = u % 2
                dve.wait_ge(x_mm, k + 1)
                dve.wait_ge(gel_done, k + 1)
                if first:
                    dve.wait_ge(small_done, e + 1)
                nc.vector.scalar_tensor_tensor(
                    t1[:, j], ps[:, 5 + 2 * j, 0:HT], small[:, par, 2 + j:3 + j], gel[:, j],
                    ALU.add, ALU.mult).then_inc(t1_done, 1)
                if not is_unit(k, 0):
                    act_lo(k - 1, (u - 1) % 4)
                dve.wait_ge(t1_done, k + 1)
                if isinstance(k, int) and k < 8:
                    weight = ones_t[:, :]
                else:
                    if first:
                        dve.wait_ge(ld_cb[par], 16 * turn)
                    weight = cb[:, par, n * HT:(n + 1) * HT]
                if not (isinstance(k, int) and k < 2):
                    dve.wait_ge(al_done, k - 1)
                nc.vector.scalar_tensor_tensor(
                    t2[:, j], t1[:, j], small[:, par, 4 + j:5 + j], weight,
                    ALU.mult, ALU.mult).then_inc(t2_done, 1)
                if is_unit(k, 1):
                    input_lo(1)
                if isinstance(k, int) and k in routing:
                    routing[k]()
                if is_unit(k, 4 * NE - 1):
                    add_input(0)

            def add_input(n):
                dve.wait_ge(y_mm, 4 * (NE - 1) + 2 * n + 2)
                for c in range(DC):
                    nc.vector.tensor_tensor(hs[:, c, n * HT:(n + 1) * HT], ps[:, 2 * n + c, 0:HT],
                                            h3[:, c, n * HT:(n + 1) * HT], ALU.add).then_inc(y_done, 1)

            over_units(dve.Fori, unit)
            act_lo(4 * NE - 1, 3)
            add_input(1)
            centre(ln4, 0, hs)
            centre(ln4, 1, hs)
            inverse_std(ln4, 0)
            inverse_std(ln4, 1)
            scale(ln4, 0)
            scale(ln4, 1)

        @block.tensor
        def _(pe):
            def keep_clock(bank, count):
                for _ in range(count):
                    mm(ps[:, bank, 0:HT], fill[:, 0:P], fill[:, :])

            def mean(ln, n, src, made, count):
                for c in range(DC):
                    pe.wait_ge(made, count - DC + c + 1)
                    last = mm(ps[:, ln.banks[n], 0:HT], ones_d, src[:, c, n * HT:(n + 1) * HT], c == 0, c == DC - 1)
                last.then_inc(ln.mean, 1)

            def var(ln, n):
                pe.wait_ge(ln.sq, n + 1)
                for c in range(DC):
                    for q in range(NQ):
                        last = mm(ps[SQ * q:SQ * (q + 1), ln.banks[n], VAR:VAR + QT], ones_d[:, 0:SQ],
                                  sq[:, n, c, q * QT:(q + 1) * QT], c == 0, c == DC - 1)
                last.then_inc(ln.var, 1)

            def spread(ln, n):
                pe.wait_ge(ln.rs, n + 1)
                for q in range(NQ):
                    last = mm(ps[:, ln.banks[n], q * QT:(q + 1) * QT], cst[:, C_SEL + q * P:C_SEL + (q + 1) * P],
                              rs[:, n])
                last.then_inc(ln.bc, 1)

            def compose(i):
                pe.wait_ge(ld_qkv[i], 32)
                pe.wait_ge(emb_done, 3 + i)
                for c in range(DC):
                    for j in range(4):
                        last = mm(ps[32 * j:32 * (j + 1), i, c * D:(c + 1) * D],
                                  vb_sb[:, i, 4 * c + j], ut_sb[:, i, 4 * c + j])
                last.then_inc(cmp_mm, 1)

            def weight_transposed(i):
                pe.wait_ge(wt_out, i + 1)
                for k in range(DC):
                    for c in range(DC):
                        last = nc.tensor.transpose(ps[:, i, k * D + c * P:k * D + (c + 1) * P],
                                                   wT[:, i, c, k * P:(k + 1) * P], ident)
                last.then_inc(wt_mm, 1)

            pe.wait_ge(fill_done, 1)
            keep_clock(7, 12)
            for k in range(KP):
                pe.wait_ge(ld_patch[k], 32)
                for n in range(NH):
                    for c in range(DC):
                        last = mm(ps[:, 2 * n + c, 0:HP], tw_sb[:, k, c * P:(c + 1) * P],
                                  pt_sb[:, k, n * HP:(n + 1) * HP], k == 0, k == KP - 1)
                        if k == KP - 1:
                            last.then_inc(emb_mm, 1)
            pe.wait_ge(ld_cst, 16)
            mean(ln1, 0, h0, emb_done, 4)
            mean(ln1, 1, h0, emb_done, 6)
            for i in range(3):
                compose(i)
            var(ln1, 0)
            var(ln1, 1)
            for i in range(3):
                weight_transposed(i)
            spread(ln1, 0)
            spread(ln1, 1)
            keep_clock(4, 4)
            pe.wait_ge(cmp_done, 3)
            pe.wait_ge(ld_out, 32)
            def projection(g):
                n, i, c = g // 6, g % 6 // 2, g % 2
                if g == 3:
                    pe.wait_ge(ln1.out, 2 * DC)
                if g in (6, 7):
                    pe.wait_ge(q_done, g - 5)
                if g in (8, 9):
                    pe.wait_ge(k_done, g - 7)
                if g in (10, 11):
                    pe.wait_ge(q_done, g - 7)
                for k in range(DC):
                    last = mm(ps[:, PROJ_BANK[g], 0:HT], wqkv[:, i, k, c * P:(c + 1) * P],
                              xn[:, k, n * HT:(n + 1) * HT], k == 0, k == DC - 1)
                last.then_inc(pr_mm, 1)

            def scores(p, par):
                pe.wait_ge(staged, p * 3 + 3)
                pe.wait_ge(k11_staged, p + 1)
                pe.wait_ge(q_staged, p + 1)
                if not (isinstance(p, int) and p < 2):
                    pe.wait_ge(s_cen, p - 1)
                for u in range(2):
                    for c in range(DC):
                        o = ps[QB * u:QB * u + S, 2 * par + c, 0:HC * S]
                        mm(o, qst[:, par, c, u * S:(u + 1) * S],
                           kblk[:, par, u, c].rearrange("p h s -> p (h s)"), True, False)
                        last = mm(o, ident_bf[0:S, :], caus_bf[0:S, :], False, True)
                last.then_inc(s_mm, 1)

            def context_transposed(p):
                pe.wait_ge(cx_done, p + 1)
                for c in range(DC):
                    last = nc.tensor.transpose(ps[:, 7, 256 + c * P:256 + c * P + QROWS],
                                               cx[0:QROWS, c * HC:(c + 1) * HC].rearrange("p h d -> p (h d)"),
                                               cst[0:QROWS, C_ID:C_ID + QROWS])
                last.then_inc(ct_mm, 1)

            pe.wait_ge(ln1.aff, 2)
            for g in range(6):
                projection(g)
            for c in range(DC):
                for k in range(2):
                    last = mm(ps[:, 3, c * D:(c + 1) * D], ou_sb[:, k, c * P:(c + 1) * P],
                              ov_sb[:, k], k == 0, k == 1)
            last.then_inc(cmp_mm, 1)
            pe.wait_ge(ln1.aff, 4)
            projection(6)
            projection(7)
            pe.wait_ge(init_done, 6)
            pe.wait_ge(vt_done, 2)
            scores(0, 0)
            projection(8)
            projection(9)
            pe.wait_ge(cmp_done, 4)
            scores(1, 1)
            projection(10)
            projection(11)
            pe.wait_ge(vt_done, 4)
            pe.wait_ge(k_done, 4)

            def output_projection(n, c):
                for k in range(DC):
                    last = mm(ps[:, OP_BANK[n] + c, 0:HT], wo[:, k, c * P:(c + 1) * P],
                              cT[:, k, n * HT:(n + 1) * HT], k == 0, k == DC - 1)
                last.then_inc(op_mm, 1)

            def turn(p, par, ahead):
                pe.wait_ge(s_exp, p + 1)
                after(pe, tr_done, p * 2)
                for g in range(NG):
                    hh = min(G3, H - g * G3)
                    at = PSLOT[g] % G3 * QROWS
                    last = nc.tensor.transpose(
                        ps[0:hh * S, 4 + PSLOT[g] // G3, at:at + QROWS],
                        prob[0:QROWS, par, g * G3:g * G3 + hh].rearrange("p h s -> p (h s)"),
                        cst[0:QROWS, C_ID:C_ID + QROWS])
                last.then_inc(tr_mm, 1)
                pe.wait_ge(v_staged, p * 4 + 4)
                after(pe, v_done, p)
                for u in range(2):
                    for c in range(DC):
                        last = nc.tensor.transpose(
                            ps[0:G3 * S, 6, u * D + c * P:u * D + (c + 1) * P],
                            vst[:, par, c, u], ident)
                last.then_inc(v_mm, 1)
                if not (isinstance(p, int) and p == 0):
                    context_transposed(p - 1)
                if ahead >= 2:
                    scores(p + 2, par)
                if ahead == 1:
                    pe.wait_ge(ct_done, PAIRS // 2)
                    output_projection(0, 0)
                if ahead == 0:
                    mean(ln2, 0, h1, op_done, 2)
                pe.wait_ge(v_done, p + 1)
                pe.wait_ge(tr_done, p * 2 + 2)
                after(pe, ct_done, p)
                for u in range(2):
                    for g in range(NG):
                        hh = min(G3, H - g * G3)
                        last = mm(ps[QB * u:QB * u + S, 7, g * G3 * DH:(g * G3 + hh) * DH],
                                  pT[0:hh * S, PSLOT[g], QB * u:QB * u + S],
                                  v3[0:hh * S, u, g * G3 * DH:(g * G3 + hh) * DH])
                last.then_inc(pv_mm, 1)

                if ahead == 1:
                    output_projection(0, 1)

            over_pairs(pe.Fori, turn)
            var(ln2, 0)
            context_transposed(PAIRS - 1)
            pe.wait_ge(ct_done, PAIRS)
            output_projection(1, 0)
            spread(ln2, 0)
            output_projection(1, 1)

            def first_low(n):
                pe.wait_ge(ln2.aff, DC * (n + 1))
                for k in range(DC):
                    last = mm(ps[:, n, 0:HT], f1u[:, k], xn[:, k, n * HT:(n + 1) * HT], k == 0, k == DC - 1)
                last.then_inc(z1_mm, 1)

            def hidden(g):
                n, f = g // FIC, g % FIC
                pe.wait_ge(z1_done, n + 1)
                if g >= 2:
                    pe.wait_ge(hm_done, g - 1)
                mm(ps[:, HM_BANK + g % 2, 0:HT], f1v[:, f * P:(f + 1) * P], z1[:, n]).then_inc(hm_mm, 1)

            def second_low(g):
                n, f = g // FIC, g % FIC
                pe.wait_ge(hm_done, g + 1)
                ins = mm(ps[:, Z2_BANK + n, 0:HT], f2u[:, f], hm[:, f], f == 0, f == FIC - 1)
                if f == FIC - 1:
                    ins.then_inc(z2_mm, 1)

            def mlp_out(n):
                pe.wait_ge(z2_done, n + 1)
                if n:
                    pe.wait_ge(mo_done, 2)
                for c in range(DC):
                    mm(ps[:, MO_BANK + c, 0:HT], f2v[:, c * P:(c + 1) * P], z2[:, n]).then_inc(mo_mm, 1)

            pe.wait_ge(ld_mlp, 64)
            first_low(0)
            mean(ln2, 1, h1, op_done, 4)
            hidden(0)
            hidden(1)
            for g in range(2, NH * FIC):
                hidden(g)
                second_low(g - 2)
                if g == 2:
                    var(ln2, 1)
                if g == 3:
                    keep_clock(1, 8)
                    spread(ln2, 1)
                if g == 5:
                    first_low(1)
                if g == 10:
                    mlp_out(0)
                if g == 11:
                    mean(ln3, 0, hs, mo_done, 2)
                if g == 13:
                    var(ln3, 0)
            second_low(NH * FIC - 2)
            second_low(NH * FIC - 1)
            keep_clock(1, 4)
            mlp_out(1)
            spread(ln3, 0)
            mean(ln3, 1, hs, mo_done, 4)
            keep_clock(3, 4)
            def logits():
                pe.wait_ge(ln3.aff, NH * DC)
                pe.wait_ge(ld_gate, 16)
                pe.wait_ge(init_done, 6)
                for t in range(TT):
                    rows = P if t < TT - 1 else LAST
                    for k in range(DC):
                        last = mm(ps[0:rows, 3, 16 * t:16 * t + E], h3[:, k, t * P:t * P + rows], gw[:, k], k == 0, k == DC - 1)
                last.then_inc(lg_mm, 1)

            def down(k, u, par, n, first=False, last_one=False):
                j = u % 2
                pe.wait_ge(al_done, k + 1)
                for c in range(DC):
                    last = weight3(lambda w: w[:, par, W1C + j * D + c * P:W1C + j * D + (c + 1) * P],
                                   ps[:, 2 * n + c, 0:HT], w_hi, w_lo, a_hi[:, u], a_lo[:, u],
                                   first, last_one)
                last.then_inc(y_mm, 1)

            def unit(k, u, e, par, turn, n, first):
                j = u % 2
                if first:
                    pe.wait_ge(w1_lo_done, e + 1)
                if is_unit(k, 1):
                    pe.wait_ge(hm_done, NH * FIC)
                if is_unit(k, 6):
                    pe.wait_ge(gt, 2)
                if not (isinstance(k, int) and k < 2):
                    pe.wait_ge(t1_done, k - 1)
                for which, done in ((1, g_mm), (0, x_mm)):
                    for c in range(DC):
                        col = c * 2 * F + which * F + j * P
                        if (is_unit(k, 0) or is_unit(k, 4)) and which:
                            pe.wait_ge(xs_lo, DC * n + c + 1)
                        last = weight3(lambda w: w[:, par, col:col + P],
                                       ps[:, 4 + 2 * j + (1 - which), 0:HT], w_hi, w_lo,
                                       x_hi[:, c, n * HT:(n + 1) * HT], x_lo[:, c, n * HT:(n + 1) * HT],
                                       c == 0, c == DC - 1)
                    last.then_inc(done, 1)
                    if is_unit(k, 1) and which:
                        spread(ln3, 1)
                if is_unit(k, 0):
                    var(ln3, 1)
                if is_unit(k, 1):
                    logits()
                if is_unit(k, 4 * (NE - 1)):
                    second_biases()
                if isinstance(k, int) and k < 2:
                    return
                if isinstance(k, int) and k < 8:
                    if k in (2, 4):
                        pe.wait_ge(w2_lo_done, k // 2)
                    down(k - 2, (u + 2) % 4, (k - 2) // 2 % 2, (k - 2) // 4, first=k in (2, 6))
                elif u < 2:
                    down(k - 2, u + 2, 1 - par, 1)
                else:
                    if u == 2:
                        pe.wait_ge(w2_lo_done, e + 1)
                    down(k - 2, u - 2, par, 0, last_one=is_unit(k, 4 * NE - 1))

            def second_biases():
                pe.wait_ge(ld_b2, 16)
                pe.wait_ge(ld_c17, 16)
                for n in range(NH):
                    for c in range(DC):
                        mm(ps[:, 2 * n + c, 0:HT], b2_sb[:, c * P:(c + 1) * P],
                           comb17[:, n * HT:(n + 1) * HT], False, False)

            over_units(pe.Fori, unit)
            down(4 * NE - 2, 2, (NE - 1) % 2, 1)
            down(4 * NE - 1, 3, (NE - 1) % 2, 1, last_one=True)
            mean(ln4, 0, hs, y_done, 2)
            mean(ln4, 1, hs, y_done, 4)
            var(ln4, 0)
            var(ln4, 1)
            spread(ln4, 0)
            spread(ln4, 1)


def _features(a):
    a = np.asarray(a)
    a = np.moveaxis(a, -1, 0)
    a = a.reshape((a.shape[0] // P, P) + a.shape[1:])
    return np.ascontiguousarray(np.moveaxis(a, 0, 1))


def kernel(**inputs):
    import concourse.bacc as bacc
    from concourse.bass_utils import run_bass_kernel_spmd as run

    a = {k.replace("L0_", ""): np.asarray(v) for k, v in inputs.items()}
    f32 = np.float32
    arrays = {}
    g = IMG // PATCH
    x = a["x"].reshape(B, CH, g, PATCH, g, PATCH).transpose(0, 2, 4, 1, 3, 5).reshape(B * NPATCH, KP * P)
    arrays["patches"] = _features(x)
    arrays["tok_w"] = _features(a["tok_W"])
    cols = [_features(a["tok_b"]), _features(a["tok_pos_embedding"][0]), _features(a["tok_cls_token"][0, 0]),
            _features(a["attn_ln1_g"]), _features(a["attn_ln1_b"]), _features(a["attn_ln2_g"]),
            _features(a["attn_ln2_b"]), _features(a["attn_q_b"].reshape(D)), _features(a["attn_k_b"].reshape(D)),
            _features(a["attn_v_b"].reshape(D)), _features(a["attn_out_b"]), _features(a["attn_fc1_b"]),
            _features(a["attn_fc2_b"])]
    arrays["vecs"] = np.concatenate([c.reshape(P, -1) for c in cols], axis=1)
    p = np.arange(P)[:, None]
    arrays["csts"] = np.concatenate([
        np.eye(P), np.full((P, P), 1.0 / D), np.repeat(p == SQ * np.arange(NQ)[None, :], P, axis=1), (p // DH == np.arange(HC)[None, :]),
        ((np.arange(DC)[None, :, None] * HC + p[:, :, None] // DH) % G3 == np.arange(G3)).reshape(P, DC * G3),
        np.where(np.tile(np.arange(S), HC)[None, :] > p, -1e9, 0.0)], axis=1).astype(f32)
    us, vs = [], []
    for w in "qkv":
        us.append(a[f"attn_{w}_U"].transpose(1, 2, 0).reshape(H // 2, 2 * R, D).transpose(1, 0, 2))
        v = a[f"attn_{w}_V"]
        blk = np.zeros((2 * R, H // 2, 2 * DH), f32)
        for i in range(2):
            blk[i * R:(i + 1) * R, :, i * DH:(i + 1) * DH] = v[i::2].transpose(1, 0, 2)
        vs.append(blk)
    arrays["ut"] = np.stack(us, axis=1)
    arrays["vblk"] = np.stack(vs, axis=1)
    arrays["out_u"] = a["attn_out_U"].T.reshape(2, RO, D).transpose(1, 0, 2)
    arrays["out_v"] = a["attn_out_V"].reshape(2, RO, D).transpose(1, 0, 2)
    arrays["fc1_u"] = a["attn_fc1_U"].reshape(DC, P, R_MLP).transpose(1, 0, 2)
    arrays["fc1_v"] = a["attn_fc1_V"]
    arrays["fc2_u"] = a["attn_fc2_U"].reshape(FIC, P, R_MLP).transpose(1, 0, 2)
    arrays["fc2_v"] = a["attn_fc2_V"]
    arrays["gate"] = _features(a["ffn_gate_w"])
    sw1 = a["ffn_s_fc1_w"].reshape(2, NS, F, D).transpose(1, 0, 2, 3).reshape(NS, 2 * F, D)
    sw2 = a["ffn_s_fc2_w"].reshape(D, NS, F).transpose(1, 0, 2)
    sb1 = a["ffn_s_fc1_b"].reshape(2, NS, F).transpose(1, 0, 2).reshape(NS, 2 * F)
    w1 = np.concatenate([sw1, a["ffn_fc1_w"]])
    w2 = np.concatenate([sw2, a["ffn_fc2_w"]])
    b1 = np.concatenate([sb1, a["ffn_fc1_b"]])
    mult = np.concatenate([a["ffn_s_geglu_mult"].reshape(NS, F), a["ffn_geglu_mult"]])
    packs = []
    for e in range(NE):
        packs.append(np.concatenate([
            w1[e].T.reshape(DC, P, 2 * F).transpose(1, 0, 2).reshape(P, W1C),
            w2[e].T.reshape(F // P, P, D).transpose(1, 0, 2).reshape(P, W2C),
            _features(b1[e][F:]).reshape(P, -1), _features(b1[e][:F]).reshape(P, -1),
            _features(mult[e]).reshape(P, -1)], axis=1))
    arrays["experts"] = np.concatenate(packs)
    arrays["b2"] = np.concatenate([a["ffn_s_fc2_b"][None], np.zeros((NS - 1, D), f32), a["ffn_fc2_b"]])
    arrays = {k: np.ascontiguousarray(v) for k, v in arrays.items()}

    nc = bacc.Bacc("TRN2", target_bir_lowering=False, num_devices=1)
    args = [nc.dram_tensor(k, v.shape, F32, kind="ExternalInput").ap() for k, v in arrays.items()]
    out = nc.dram_tensor("out", (D, T), F32, kind="ExternalOutput").ap()
    comb_dram = nc.dram_tensor("comb_dram", (NE, TPAD), F32, kind="Internal").ap()
    vit_tower_kernel(nc, *args, out, comb_dram)
    r = run(nc, [arrays], core_ids=[0])
    return np.ascontiguousarray(r.results[0]["out"].T.reshape(B, S, D))
```
